# Optimizing a Trainium2 kernel written in Bass

```python
import numpy as np
import jax
import jax.numpy as jnp

def _softmax(x, axis=-1):
    return jax.nn.softmax(x, axis=axis)

def _gelu(x):
    return jax.nn.gelu(x, approximate=True)

def _silu(x):
    return jax.nn.silu(x)

def _sigmoid(x):
    return jax.nn.sigmoid(x)

def _layernorm(x, axis=-1, eps=1e-05):
    m = jnp.mean(x, axis=axis, keepdims=True)
    v = jnp.var(x, axis=axis, keepdims=True)
    return (x - m) / jnp.sqrt(v + eps)

def _scatter_add(tgt, idx, src, axis=0):
    return tgt.at[idx].add(src)

def _segment_sum(src, seg, n):
    return jax.ops.segment_sum(src, seg, n)
kernel_name = 'mk_adj_preln_d1_adj_r2_308707'

def setup_inputs(seed: int=0):
    np.random.seed(seed)
    _w = jnp.asarray

    def _rec_inputs():
        import jax
        import jax.numpy as jnp
        _gk = jax.random.key(seed)
        x = -0.0005146 + 1 * jax.random.normal(jax.random.fold_in(_gk, 1), (8, 1024, 128), jnp.float32)
        _a = jax.random.bernoulli(jax.random.fold_in(_gk, 2), 0.00195312, (8, 1024, 1024))
        _a = jnp.logical_or(_a, jnp.swapaxes(_a, -1, -2))
        _a = jnp.logical_or(_a, jnp.eye(1024, dtype=bool))
        adj = _a.astype(jnp.int32)
        return (x, adj)
    x, adj = _rec_inputs()

    def _L0_gnn_setup():
        import jax, jax.numpy as jnp
        import numpy as np
        B, N, C, OUT, S = (4, 1024, 128, 128, 25)
        DENSITY = 0.008
        key = jax.random.key(seed)
        kA, kX, kW = jax.random.split(key, 3)
        A = jax.random.bernoulli(kA, DENSITY, (B, N, N)).astype(jnp.int32)
        X = jax.random.normal(kX, (B, N, C), dtype=jnp.float32)
        W = jax.random.normal(kW, (2 * C, OUT), dtype=jnp.float32) * np.float32(1.0 / np.sqrt(2 * C))
        b = jnp.zeros((OUT,), dtype=jnp.float32)
        return {'A': A, 'X': X, 'W': W, 'b': b}
    _L0_gnn_all = _L0_gnn_setup()
    _L0_gnn_in = {k: v for k, v in _L0_gnn_all.items() if k in ('W', 'b')}
    del _L0_gnn_all
    return {'x': x, 'adj': adj, 'L0_gnn_W': _L0_gnn_in['W'], 'L0_gnn_b': _L0_gnn_in['b']}

def reference(x, adj, L0_gnn_W, L0_gnn_b):
    import jax
    import jax.numpy as jnp

    def _L0_gnn_ref(A, X, W, b):
        import jax, jax.numpy as jnp
        import numpy as np
        B, N, C, OUT, S = (4, 1024, 128, 128, 25)
        DENSITY = 0.008
        mask = A != 0
        neg_inf = jnp.float32(-jnp.inf)
        pri = -jnp.arange(N, dtype=jnp.float32)
        scores = jnp.where(mask, pri, neg_inf)
        vals, idx = jax.lax.top_k(scores, S)
        valid = vals > neg_inf
        feats = jax.vmap(lambda x, i: x[i])(X, idx)
        feats = jnp.where(valid[..., None], feats, neg_inf)
        agg = feats.max(axis=2)
        degree = mask.sum(axis=-1)
        agg = jnp.where((degree <= S)[..., None], jnp.maximum(agg, 0.0), agg)
        h = jnp.concatenate([X, agg], axis=-1)
        out = jax.nn.relu(jnp.einsum('bnf,fo->bno', h, W) + b)
        return out
    h = jnp.maximum(_layernorm(x, axis=-1), 0.0)
    x = x + _L0_gnn_ref(adj, h, L0_gnn_W, L0_gnn_b)
    return x

_drawn_inputs = setup_inputs


def setup_inputs(seed=0):
    import zlib

    import numpy as np

    out = dict(_drawn_inputs(seed))
    spreads = {'L0_gnn_b': (0.0, 0.1)}
    factors = {}
    for name, (base, spread) in spreads.items():
        noise = np.random.default_rng([zlib.crc32(name.encode()), seed]).standard_normal(out[name].shape)
        drawn = base * np.exp(spread * noise) if base else spread * noise
        out[name] = jnp.asarray(drawn.astype(out[name].dtype))
    for name, factor in factors.items():
        out[name] = (out[name] * factor).astype(out[name].dtype)
    return out
```

```python
import concourse.bass as bass
from concourse import mybir
from contextlib import ExitStack

F32 = mybir.dt.float32
BF16 = mybir.dt.bfloat16
I32 = mybir.dt.int32
ALU = mybir.AluOpType
ACT = mybir.ActivationFunctionType
AX = mybir.AxisListType

P = 128
EPS = 1e-5
KEEP = 25
STATIC = 3
AHEAD = 3
MARK = 128.0
CUT = -4096.0
SEL = 4
PARTS = 3


def gnn_layer(nc, x, adj, w, b, out):
    B, N, C = x.shape
    NQ = N // P
    NT = 4
    GN = NT * P
    G = B * N // GN

    adj_g = adj.rearrange("b (g t p) m -> p (b g) t m", t=NT, p=P)
    x_g = x.rearrange("b (g t p) c -> p (b g) t c", t=NT, p=P)
    out_g = out.rearrange("b (g t p) c -> p (b g) t c", t=NT, p=P)

    ctx = ExitStack()
    with ctx:
        def sb(name, shape, dt):
            return ctx.enter_context(nc.sbuf_tensor(name, shape, dt))

        def pb(name, shape, dt):
            return ctx.enter_context(nc.psum_tensor(name, shape, dt))

        def sem(name):
            return ctx.enter_context(nc.semaphore(name))

        adj_i = sb("adj_i", [P, 2, NT, N], I32)
        adj_a = sb("adj_a", [P, 2, NT, N], BF16)
        maskT = sb("maskT", [P, 2, NQ, GN], BF16)
        rank = sb("rank", [P, 2, NQ, GN], BF16)
        pick = sb("pick", [P, 2, STATIC, GN], BF16)
        pick_more = sb("pick_more", [P, SEL, GN], BF16)
        xs = sb("xs", [P, G, NT, C], F32)
        h32 = sb("h32", [P, 2, NT, C], F32)
        hpart = sb("hpart", [P, 2, 2, PARTS, NT, C], BF16)
        hrest = sb("hrest", [P, NT, C], F32)
        hT = sb("hT", [P, 2, GN], F32)
        agg = sb("agg", [P, 2, GN], F32)
        y = sb("y", [P, 2, NT, C], F32)
        stats = sb("stats", [P, NT, 6], F32)
        mv = sb("mv", [P, NT, 2], F32)
        std = sb("std", [P, NT], F32)
        rstd = sb("rstd", [P, NT], F32)
        nmr = sb("nmr", [P, NT], F32)
        eps_t = sb("eps_t", [P, 1], F32)
        w_t = sb("w_t", [P, 2, C], F32)
        b_t = sb("b_t", [1, C], F32)
        ones_row = sb("ones_row", [1, P], F32)
        id_b = sb("id_b", [P, P], BF16)
        id_f = sb("id_f", [P, P], F32)
        tri_rank = sb("tri_rank", [P, P], BF16)
        tri_cut = sb("tri_cut", [P, P], BF16)
        ones_b = sb("ones_b", [P, P], BF16)
        count_w = sb("count_w", [P, NQ, NQ + 1], BF16)
        level_f = sb("level_f", [P, P], F32)
        most = sb("most", [NQ + 1, 1], F32)
        more = sb("more", [1, 2, 32], I32)
        MORE, NEXT, LATE, LONG = 0, NQ, 2 * NQ, 3 * NQ

        got = [pb(f"got{j}", [P, GN], F32) for j in range(STATIC)]
        got_more = pb("got_more", [P, 2, GN], F32)
        flip = pb("flip", [P, GN], BF16)
        prefix = pb("prefix", [P, GN], F32)
        misc = pb("misc", [P, GN], F32)

        adj_in = [sem("adj_in0"), sem("adj_in1")]
        x_in = sem("x_in")
        w_in = sem("w_in")
        consts = sem("consts")
        consts_b = sem("consts_b")
        abs_done = sem("abs_done")
        flip_done = sem("flip_done")
        mask_done = sem("mask_done")
        prefix_done = sem("prefix_done")
        rank_done = sem("rank_done")
        pick_done = sem("pick_done")
        got_done = sem("got_done")
        max_done = sem("max_done")
        sel_done = sem("sel_done")
        more_got = sem("more_got")
        more_max = sem("more_max")
        agg_done = sem("agg_done")
        count_done = sem("count_done")
        most_done = sem("most_done")
        most_row = sem("most_row")
        more_done = sem("more_done")
        cut_prefix = sem("cut_prefix")
        cut_mask = sem("cut_mask")
        hT_psum = sem("hT_psum")
        hT_done = sem("hT_done")
        fin_done = sem("fin_done")
        y_done = sem("y_done")
        out_st = [sem("out_st0"), sem("out_st1")]
        passed = sem("passed")
        ln = sem("ln")
        std_done = sem("std_done")
        h_done = sem("h_done")
        split = sem("split")
        LN_OPS = 2 * NT + 2
        CONSTS = 6

        block = ctx.enter_context(nc.Block())

        def wait(eng, s, v):
            if not isinstance(v, int) or v > 0:
                eng.wait_ge(s, v)

        def wait_apart(eng, s, v):
            wait(eng, s, v)
            if not isinstance(v, int):
                eng.sem_inc(passed, 1)

        def groups(eng, body):
            for k in (0, 1):
                body(k, k % 2, (k // 2) % 2, k)
            with eng.Fori(1, G // 2 - 2) as i:
                for par in (0, 1):
                    body(2 * i + par, par, i % 2, None)
            for k in range(G - 4, G):
                body(k, k % 2, (k // 2) % 2, k)

        scratch = {}

        def again(eng, value, least, most_):
            if isinstance(value, int):
                return value
            if (eng, least) not in scratch:
                scratch[eng, least] = eng.alloc_register(f"again{least}")
            eng.reg_mov(scratch[eng, least], value)
            return eng.snap(scratch[eng, least], min_val=least, max_val=most_)

        def ahead(fixed, n):
            return fixed is None or fixed + n < G

        @block.sync
        def _(sp):
            def load_adj(g, par):
                wait(sp, abs_done, NT * (g - 1))
                sp.dma_start(adj_i[:, par, :, :], adj_g[:, bass.ds(g, 1), :, :].rearrange("p g t m -> p (g t) m")).then_inc(adj_in[par], 16)

            def load_x(g):
                sp.wait_ge(x_in, 16 * (g - 3))
                sp.dma_start(xs[:, bass.ds(g, 1), :, :].rearrange("p g t c -> p (g t) c"),
                             x_g[:, bass.ds(g, 1), :, :].rearrange("p g t c -> p (g t) c")).then_inc(x_in, 16)

            sp.dma_start(xs[:, 0:4, :, :], x_g[:, 0:4, :, :]).then_inc(x_in, 16)
            load_adj(0, 0)
            load_adj(1, 1)
            sp.dma_start(w_t[:, :, :], w.rearrange("(two p) o -> p two o", p=P)).then_inc(w_in, 16)
            sp.dma_start(b_t[0:1, :], b.rearrange("(one o) -> one o", one=1)).then_inc(w_in, 16)
            load_adj(2, 0)
            load_adj(3, 1)

            def body(k, par, bp, fixed):
                if ahead(fixed, 4):
                    load_adj(k + 4, par)
                    load_x(k + 4)
                if fixed is None or fixed > 0:
                    sp.wait_ge(y_done, k)
                    sp.dma_start(out_g[:, bass.ds(k - 1, 1), :, :].rearrange("p g t c -> p (g t) c"), y[:, 1 - par, :, :]).then_inc(out_st[1 - par], 16)

            groups(sp, body)
            sp.wait_ge(y_done, G)
            sp.dma_start(out_g[:, G - 1, :, :], y[:, (G - 1) % 2, :, :]).then_inc(out_st[(G - 1) % 2], 16)
            for par in (0, 1):
                sp.wait_ge(out_st[par], 8 * G)

        @block.gpsimd
        def _(pool):
            g = nc.gpsimd
            g.memset(id_b[:], 0.0).then_inc(consts_b, 1)
            g.memset(tri_rank[:], 0.0).then_inc(consts_b, 1)
            g.memset(tri_cut[:], 0.0).then_inc(consts_b, 1)
            g.memset(id_f[:], 0.0).then_inc(consts_b, 1)
            g.memset(count_w[:], 0.0).then_inc(consts_b, 1)
            pool.wait_ge(consts_b, 5)
            for t, v in ((id_b, 1.0), (tri_rank, MARK), (tri_cut, CUT), (id_f, 1.0)):
                g.affine_select(out=t[:], in_=t[:], compare_op=ALU.not_equal, fill=v, base=0,
                                pattern=[[-1, P]], channel_multiplier=1).then_inc(consts_b, 1)
            for q in range(NQ):
                g.memset(count_w[:, q, q:q + 1], 1.0)
                last = g.memset(count_w[:, q, NQ:NQ + 1], 1.0)
            last.then_inc(consts_b, 1)
            pool.wait_ge(consts_b, 10)
            for t in (tri_rank, tri_cut):
                g.affine_select(out=t[:], in_=t[:], compare_op=ALU.is_ge, fill=1.0, base=0,
                                pattern=[[-1, P]], channel_multiplier=1).then_inc(consts, 1)
            g.memset(ones_b[:], 1.0).then_inc(consts, 1)
            g.memset(ones_row[:], 1.0).then_inc(consts, 1)
            g.memset(eps_t[:], EPS).then_inc(consts, 1)
            g.iota(level_f[:], pattern=[[1, P]], base=int(MARK) + STATIC, channel_multiplier=0,
                   allow_small_or_imprecise_dtypes=True).then_inc(consts, 1)

            def body(group, par, bp, fixed):
                k = again(pool, group, 2, G - 5)
                for q in range(NQ):
                    k = again(pool, group, 2, G - 5)
                    wait_apart(pool, rank_done, NQ * k + q + 1)
                    for j in range(STATIC):
                        wait_apart(pool, got_done, STATIC * (NQ * k + q - 2) + j + 1)
                        g.tensor_scalar(pick[:, q % 2, j, :], rank[:, par, q, :], MARK + j, None,
                                        ALU.is_equal).then_inc(pick_done, 1)

            groups(pool, body)

        @block.scalar
        def _(act):
            def absolute(g, par, t):
                act.wait_ge(adj_in[par], 16 * ((g - par) // 2 + 1) if isinstance(g, int) else 8 * (g - par) + 16)
                wait(act, flip_done, NQ * (g - 1))
                nc.scalar.activation(adj_a[:, par, t, :], adj_i[:, par, t, :], ACT.Abs).then_inc(abs_done, 1)

            def mask(g, par, q):
                act.wait_ge(flip_done, NQ * g + q + 1)
                wait(act, prefix_done, NQ * (g - 1))
                nc.scalar.activation(maskT[:, par, q, :], flip[:], ACT.Sign).then_inc(mask_done, 1)

            def ranks(g, par, q):
                act.wait_ge(prefix_done, NQ * g + q + 1)
                wait(act, pick_done, STATIC * NQ * (g - 1))
                wait(act, agg_done, g - 1)
                nc.scalar.copy(rank[:, par, q, :], prefix[:]).then_inc(rank_done, 1)

            def deviation(g):
                act.wait_ge(ln, LN_OPS * g + 2 * NT)
                nc.scalar.activation(std[:], mv[:, :, 1], ACT.Sqrt, bias=eps_t[:, 0:1]).then_inc(std_done, 1)

            def normalise(g, par, g_x):
                act.wait_ge(ln, LN_OPS * (g + 1))
                wait(act, hT_psum, g - 1)
                for t in range(NT):
                    nc.scalar.activation(h32[:, par, t, :], xs[:, bass.ds(g_x, 1), t, :].rearrange("p g c -> p (g c)"), ACT.Relu,
                                         bias=nmr[:, t:t + 1], scale=rstd[:, t:t + 1]).then_inc(h_done, 1)

            for t in range(NT):
                absolute(0, 0, t)
            for g in (0, 1):
                if g == 0:
                    act.wait_ge(consts, CONSTS)
                deviation(g)
                normalise(g, g, g)
            for q in range(NQ):
                mask(0, 0, q)
                if q < NT:
                    absolute(1, 1, q)
            for q in range(NQ):
                ranks(0, 0, q)
                mask(1, 1, q)
                if q < NT:
                    absolute(2, 0, q)

            def body(group, par, bp, fixed):
                k = again(act, group, 2, G - 5)
                for q in range(NQ):
                    k = again(act, group, 2, G - 5)
                    if q >= NQ // 2 and ahead(fixed, 1):
                        ranks(k + 1, 1 - par, 2 * q - NQ)
                    if q == 5 and ahead(fixed, 2):
                        deviation(k + 2)
                    if ahead(fixed, 2):
                        mask(k + 2, par, q)
                    if q < NT and ahead(fixed, 3):
                        absolute(k + 3, 1 - par, q)
                    if q >= NQ // 2 and ahead(fixed, 1):
                        ranks(k + 1, 1 - par, 2 * q - NQ + 1)
                    if q == 6 and ahead(fixed, 2):
                        normalise(k + 2, par, k + 2)

            groups(act, body)

        @block.tensor
        def _(pe):
            pe.sem_inc(more_got, SEL)
            further = pe.alloc_register("pe_further")
            pe.reg_mov(further, 0)
            cuts = pe.alloc_register("pe_cuts")
            pe.reg_mov(cuts, 0)
            counts = [pe.alloc_register(f"pe_more{q}") for q in range(NQ)]
            cut_flag = pe.alloc_register("pe_cut_flag")

            def transpose(g, par, q):
                pe.wait_ge(abs_done, NT * (g + 1))
                wait(pe, mask_done, NQ * g + q)
                for t in range(NT):
                    last = nc.tensor.transpose(flip[:, t * P:(t + 1) * P],
                                               adj_a[:, par, t, q * P:(q + 1) * P], id_b[:])
                last.then_inc(flip_done, 1)

            def number(g, par, q):
                pe.wait_ge(mask_done, NQ * g + q + 1)
                wait(pe, rank_done, NQ * g + q)
                nc.tensor.matmul(prefix[:], tri_rank[:], maskT[:, par, q, :], start=True, stop=True).then_inc(prefix_done, 1)

            def count(g, par):
                pe.wait_ge(mask_done, NQ * (g + 1))
                wait(pe, hT_done, g - 1)
                for q in range(NQ):
                    last = nc.tensor.matmul(misc[0:NQ + 1, :], count_w[:, q, :], maskT[:, par, q, :],
                                            start=(q == 0), stop=(q == NQ - 1))
                last.then_inc(count_done, 1)

            def count_row(g):
                wait_apart(pe, most_done, g + 1)
                nc.tensor.matmul(misc[0:1, 0:NQ + 1], most[:, 0:1], id_f[0:NQ + 1, 0:NQ + 1],
                                 start=True, stop=True).then_inc(most_row, 1)

            def cut(g, par):
                pe.wait_ge(more_done, 4 * (g + 1))
                wait_apart(pe, rank_done, NQ * g)
                pe.reg_load(cut_flag, more[0:1, par, LONG:LONG + 1])
                with pe.If(pe.snap(cut_flag, min_val=0, max_val=N)):
                    done = pe.snap(cuts, min_val=0, max_val=NQ * G)
                    for n, q in enumerate(range(NQ - 1, -1, -1)):
                        if n:
                            pe.wait_ge(cut_mask, done + n)
                        for before in range(q):
                            nc.tensor.matmul(prefix[:], ones_b[:], maskT[:, par, before, :], start=(before == 0), stop=False)
                        nc.tensor.matmul(prefix[:], tri_cut[:], maskT[:, par, q, :], start=(q == 0), stop=True).then_inc(cut_prefix, 1)
                    pe.wait_ge(cut_mask, done + NQ)
                    pe.reg_add(cuts, cuts, NQ)
                pe.nop()

            def load_counts(g, par):
                wait_apart(pe, more_done, 4 * (g + 1))
                pe.load(counts, more[0:1, par, MORE:MORE + NQ])

            def product(dst, hp, onehot, sem_):
                for part in range(PARTS):
                    last = nc.tensor.matmul(dst, hp[part], onehot, start=(part == 0), stop=(part == PARTS - 1))
                last.then_inc(sem_, 1)

            def gather(k, par, hp, q):
                for j in range(STATIC):
                    item = STATIC * (NQ * k + q) + j
                    pe.wait_ge(pick_done, item + 1)
                    wait(pe, max_done, item + 1 - STATIC)
                    product(got[j][:], hp, pick[:, q % 2, j, :], got_done)
                n = pe.snap(counts[q], min_val=0, max_val=P - STATIC)
                with pe.If(n):
                    with pe.Fori(0, n):
                        d = pe.snap(further, min_val=0, max_val=G * NQ * P)
                        pe.wait_ge(sel_done, d + 1)
                        pe.wait_ge(more_max, d + 1)
                        product(got_more[:, bass.ds(d % 2, 1), :], hp, pick_more[:, bass.ds(d % SEL, 1), :], more_got)
                        pe.reg_add(further, further, 1)
                    pe.nop()

            def turn_h(g, par):
                pe.wait_ge(h_done, NT * (g + 1))
                wait(pe, y_done, g)
                pe.wait_ge(more_done, 4 * (g + 1))
                for t in range(NT):
                    last = nc.tensor.transpose(misc[:, t * P:(t + 1) * P], h32[:, par, t, :], id_f[:])
                last.then_inc(hT_psum, 1)

            def finish(g, par):
                pe.wait_ge(agg_done, g + 1)
                pe.wait_ge(hT_done, g + 1)
                if isinstance(g, int) and g == 0:
                    pe.wait_ge(w_in, 32)
                for t in range(NT):
                    o = misc[:, t * P:(t + 1) * P]
                    nc.tensor.matmul(o, hT[:, par, t * P:(t + 1) * P], w_t[:, 0, :], start=True, stop=False)
                    nc.tensor.matmul(o, agg[:, par, t * P:(t + 1) * P], w_t[:, 1, :], start=False, stop=False)
                    last = nc.tensor.matmul(o, ones_row[0:1, :], b_t[0:1, :], start=False, stop=True)
                last.then_inc(fin_done, 1)

            pe.wait_ge(consts, CONSTS)
            for q in range(NQ):
                transpose(0, 0, q)
            count(0, 0)
            count_row(0)
            cut(0, 0)
            for q in range(NQ):
                number(0, 0, q)
                transpose(1, 1, q)

            def body(group, par, bp, fixed):
                k = again(pe, group, 2, G - 5)
                def parts(q):
                    if isinstance(bp, int):
                        return [hpart[:, bp, q // NT, part, q % NT, :] for part in range(PARTS)]
                    now = bass.ds(again(pe, bp, 0, 1), 1)
                    return [hpart[:, now, q // NT, part, q % NT, :].rearrange("p b c -> p (b c)") for part in range(PARTS)]

                load_counts(k, par)
                pe.wait_ge(split, 4 * (k - par + 2))
                for q in range(NQ):
                    k = again(pe, group, 2, G - 5)
                    if q >= NQ // 2 and ahead(fixed, 1):
                        number(k + 1, 1 - par, 2 * q - NQ)
                    gather(k, par, parts(q), q)
                    if ahead(fixed, 2):
                        transpose(k + 2, par, q)
                    if q >= NQ // 2 and ahead(fixed, 1):
                        number(k + 1, 1 - par, 2 * q - NQ + 1)
                    if q == 0 and ahead(fixed, 1):
                        count(k + 1, 1 - par)
                    if q == 1 and ahead(fixed, 1):
                        count_row(k + 1)
                    if q == 2 and (fixed is None or fixed > 0):
                        if ahead(fixed, 1):
                            pe.wait_ge(more_done, 4 * (k + 2))
                        finish(k - 1, 1 - par)
                    if q == 3:
                        turn_h(k, par)
                        if ahead(fixed, 1):
                            cut(k + 1, 1 - par)

            groups(pe, body)
            finish(G - 1, (G - 1) % 2)

        @block.vector
        def _(dve):
            v = nc.vector
            dve.sem_inc(more_max, 2)
            sel = dve.alloc_register("dve_sel")
            dve.reg_mov(sel, 0)
            further = dve.alloc_register("dve_further")
            dve.reg_mov(further, 0)
            cuts = dve.alloc_register("dve_cuts")
            dve.reg_mov(cuts, 0)
            soon = [dve.alloc_register(f"dve_next{q}") for q in range(NQ)]
            late = [dve.alloc_register(f"dve_late{q}") for q in range(NQ)]
            cut_flag = dve.alloc_register("dve_cut_flag")

            def moments(g, g_x):
                dve.wait_ge(x_in, 16 * (max(g, 3) - 2) if isinstance(g, int) else 16 * (g - 2))
                for t in range(NT):
                    v.bn_stats(stats[:, t, :], xs[:, bass.ds(g_x, 1), t, :].rearrange("p g c -> p (g c)")).then_inc(ln, 1)
                for t in range(NT):
                    wait_apart(dve, ln, LN_OPS * g + t + 1)
                    v.bn_aggr(mv[:, t, :], stats[:, t, :]).then_inc(ln, 1)

            def scale_bias(g):
                dve.wait_ge(std_done, g + 1)
                wait(dve, h_done, NT * g)
                v.reciprocal(rstd[:], std[:]).then_inc(ln, 1)
                dve.wait_ge(ln, LN_OPS * g + 2 * NT + 1)
                v.scalar_tensor_tensor(nmr[:], mv[:, :, 0], -1.0, rstd[:], ALU.mult, ALU.mult).then_inc(ln, 1)

            def split_h(g, par, bp):
                dve.wait_ge(h_done, NT * (g + 1))
                src = h32[:, par, :, :]

                def part(n):
                    if isinstance(bp, int):
                        return hpart[:, bp, par, n, :, :]
                    return hpart[:, bass.ds(bp, 1), par, n, :, :].rearrange("p b t c -> p (b t) c")
                v.tensor_copy(part(0), src).then_inc(split, 1)
                dve.wait_ge(split, 4 * g + 1)
                v.tensor_tensor(hrest[:], src, part(0), ALU.subtract).then_inc(split, 1)
                dve.wait_ge(split, 4 * g + 2)
                v.tensor_copy(part(1), hrest[:]).then_inc(split, 1)
                dve.wait_ge(split, 4 * g + 3)
                v.tensor_tensor(part(2), hrest[:], part(1), ALU.subtract).then_inc(split, 1)

            def most_of(g):
                dve.wait_ge(count_done, g + 1)
                v.reduce_max(most[:, 0:1], misc[0:NQ + 1, :], AX.X).then_inc(most_done, 1)

            def loop_counts(g, par):
                dve.wait_ge(most_row, g + 1)
                m = more[0:1, par, :]
                v.tensor_scalar(m[:, MORE:MORE + NQ], misc[0:1, 0:NQ], float(-STATIC), 0.0, ALU.add, ALU.max).then_inc(more_done, 1)
                v.tensor_scalar(m[:, LONG:LONG + 1], misc[0:1, NQ:NQ + 1], float(-KEEP), 0.0, ALU.add, ALU.max).then_inc(more_done, 1)
                dve.wait_ge(more_done, 4 * g + 1)
                v.tensor_scalar(m[:, NEXT:NEXT + NQ], m[:, MORE:MORE + NQ], float(AHEAD), None, ALU.min).then_inc(more_done, 1)
                v.tensor_scalar(m[:, LATE:LATE + NQ], m[:, MORE:MORE + NQ], float(-AHEAD), 0.0, ALU.add, ALU.max).then_inc(more_done, 1)

            def cut(g, par):
                wait_apart(dve, more_done, 4 * (g + 1))
                dve.reg_load(cut_flag, more[0:1, par, LONG:LONG + 1])
                with dve.If(dve.snap(cut_flag, min_val=0, max_val=N)):
                    done = dve.snap(cuts, min_val=0, max_val=NQ * G)
                    for n, q in enumerate(range(NQ - 1, -1, -1)):
                        dve.wait_ge(cut_prefix, done + n + 1)
                        v.tensor_scalar(maskT[:, par, q, :], prefix[:], CUT + KEEP - 1, None, ALU.is_le).then_inc(cut_mask, 1)
                    dve.reg_add(cuts, cuts, NQ)
                dve.nop()

            def load_counts(g, par):
                wait_apart(dve, more_done, 4 * (g + 1))
                dve.load(soon, more[0:1, par, NEXT:NEXT + NQ])
                dve.load(late, more[0:1, par, LATE:LATE + NQ])

            def select(par, q, level):
                s = dve.snap(sel, min_val=0, max_val=G * NQ * P)
                dve.wait_ge(more_got, s + 1)
                v.tensor_scalar(pick_more[:, bass.ds(s % SEL, 1), :], rank[:, par, q:q + 1, :],
                                level_f[:, bass.ds(level, 1)], None, ALU.is_equal).then_inc(sel_done, 1)
                dve.reg_add(sel, sel, 1)

            def fold(par):
                d = dve.snap(further, min_val=0, max_val=G * NQ * P)
                dve.wait_ge(more_got, d + 1 + SEL)
                dve.wait_ge(more_max, d + 2)
                v.tensor_tensor(agg[:, par:par + 1, :], agg[:, par:par + 1, :], got_more[:, bass.ds(d % 2, 1), :],
                                ALU.max).then_inc(more_max, 1)
                dve.reg_add(further, further, 1)

            def maxima(k, par, q):
                n = dve.snap(soon[q], min_val=0, max_val=AHEAD)
                with dve.If(n):
                    wait_apart(dve, rank_done, NQ * k + q + 1)
                    with dve.Fori(0, n) as j:
                        select(par, q, j)
                    dve.nop()
                for j in range(STATIC):
                    item = STATIC * (NQ * k + q) + j
                    dve.wait_ge(got_done, item + 1)
                    if q == 0 and j == 0:
                        v.tensor_scalar(agg[:, par, :], got[j][:], 0.0, None, ALU.max).then_inc(max_done, 1)
                        continue
                    dve.wait_ge(max_done, item)
                    if j == 0:
                        dve.wait_ge(more_max, dve.snap(further, min_val=0, max_val=G * NQ * P) + 2)
                    v.tensor_tensor(agg[:, par, :], agg[:, par, :], got[j][:], ALU.max).then_inc(max_done, 1)
                with dve.If(n):
                    wait_apart(dve, max_done, STATIC * (NQ * k + q + 1))
                    with dve.Fori(0, n):
                        fold(par)
                    dve.nop()
                r = dve.snap(late[q], min_val=0, max_val=P - STATIC - AHEAD)
                with dve.If(r):
                    with dve.Fori(0, r) as j:
                        select(par, q, j + AHEAD)
                        fold(par)
                    dve.nop()

            def turned_h(g, par):
                dve.wait_ge(hT_psum, g + 1)
                v.tensor_copy(hT[:, par, :], misc[:]).then_inc(hT_done, 1)

            def output(g, par, g_x):
                dve.wait_ge(fin_done, g + 1)
                if isinstance(g, int):
                    wait(dve, out_st[par], 16 * (g // 2))
                else:
                    dve.wait_ge(out_st[par], 8 * (g - par))
                v.scalar_tensor_tensor(y[:, par, :, :], misc[:].rearrange("p (t c) -> p t c", t=NT), 0.0,
                                       xs[:, bass.ds(g_x, 1), :, :].rearrange("p g t c -> p (g t) c"), ALU.max, ALU.add).then_inc(y_done, 1)

            for g in (0, 1):
                moments(g, g)
                scale_bias(g)
                split_h(g, g, 0)
            most_of(0)
            loop_counts(0, 0)
            cut(0, 0)

            def body(group, par, bp, fixed):
                k = again(dve, group, 2, G - 5)
                load_counts(k, par)
                for q in range(NQ):
                    k = again(dve, group, 2, G - 5)
                    maxima(k, par, q)
                    if q == 0 and ahead(fixed, 1):
                        most_of(k + 1)
                    if q == 1 and ahead(fixed, 1):
                        loop_counts(k + 1, 1 - par)
                    if q == 2 and (fixed is None or fixed > 0):
                        output(k - 1, 1 - par, k - 1)
                    if q == 3:
                        turned_h(k, par)
                        if ahead(fixed, 1):
                            cut(k + 1, 1 - par)
                    if ahead(fixed, 2):
                        if q == 4:
                            moments(k + 2, k + 2)
                        if q == 6:
                            scale_bias(k + 2)
                        if q == 7:
                            split_h(k + 2, par, 1 - bp)
                dve.wait_ge(max_done, STATIC * NQ * (k + 1))
                dve.wait_ge(more_max, dve.snap(further, min_val=0, max_val=G * NQ * P) + 2)
                dve.sem_inc(agg_done, 1)

            groups(dve, body)
            output(G - 1, (G - 1) % 2, G - 1)


_INS = ['x', 'adj', 'L0_gnn_W', 'L0_gnn_b']
_OUTS = [((8, 1024, 128), 'float32')]


def kernel(**inputs):
    import numpy as _np
    import concourse.bacc as _bacc
    from concourse import mybir as _mybir
    from concourse.bass_utils import run_bass_kernel_spmd as _run

    nc = _bacc.Bacc("TRN2", target_bir_lowering=False, num_devices=1)
    arrays, args = {}, []
    for name in _INS:
        a = _np.ascontiguousarray(inputs[name])
        arrays[f"in_{name}_dram"] = a
        args.append(nc.dram_tensor(f"in_{name}_dram", a.shape, _mybir.dt.from_np(a.dtype), kind="ExternalInput").ap())
    for i, (shape, dtype) in enumerate(_OUTS):
        dt = _mybir.dt.from_np(_np.dtype(dtype))
        args.append(nc.dram_tensor(f"out_{i}_dram", shape, dt, kind="ExternalOutput").ap())
    gnn_layer(nc, *args)
    r = _run(nc, [arrays], core_ids=[0])
    got = tuple(r.results[0][f"out_{i}_dram"] for i in range(len(_OUTS)))
    return got[0]
```

```python
import concourse.bass as bass
from concourse import mybir
from contextlib import ExitStack

F32 = mybir.dt.float32
BF16 = mybir.dt.bfloat16
I32 = mybir.dt.int32
ALU = mybir.AluOpType
ACT = mybir.ActivationFunctionType
AX = mybir.AxisListType

P = 128
EPS = 1e-5
KEEP = 25
STATIC = 4
PAIR = 2
MARK = 128.0
CUT = -4096.0
SEL = 4
PARTS = 3


def gnn_layer(nc, x, adj, w, b, out):
    B, N, C = x.shape
    NQ = N // P
    NT = 4
    GN = NT * P
    HQ = NQ // 2
    G = B * N // GN
    NP = STATIC // PAIR
    XB = 8

    adj_g = adj.rearrange("b (g t p) m -> p (b g) t m", t=NT, p=P)
    x_g = x.rearrange("b (g t p) c -> p (b g) t c", t=NT, p=P)
    out_g = out.rearrange("b (g t p) c -> p (b g) t c", t=NT, p=P)

    ctx = ExitStack()
    with ctx:
        def sb(name, shape, dt):
            return ctx.enter_context(nc.sbuf_tensor(name, shape, dt))

        def pb(name, shape, dt):
            return ctx.enter_context(nc.psum_tensor(name, shape, dt))

        def sem(name):
            return ctx.enter_context(nc.semaphore(name))

        adj_i = sb("adj_i", [P, 2, NT, N], I32)
        adj_a = sb("adj_a", [P, 2, NT, N], BF16)
        maskT = sb("maskT", [P, 2, NQ, GN], BF16)
        rank = sb("rank", [P, 2, NQ, GN], BF16)
        pick = sb("pick", [P, 2, STATIC, HQ, GN], BF16)
        pick_more = sb("pick_more", [P, SEL, GN], BF16)
        xs = sb("xs", [P, XB, NT, C], F32)
        h32 = sb("h32", [P, 2, NT, C], F32)
        hpart = sb("hpart", [P, 2, NQ, PARTS, C], BF16)
        hrest = sb("hrest", [P, NT, C], F32)
        hT = sb("hT", [P, 2, GN], F32)
        acc = sb("acc", [P, NP, PAIR, GN], F32)
        agg = sb("agg", [P, 2, GN], F32)
        y = sb("y", [P, 2, NT, C], F32)
        stats = sb("stats", [P, NT, 6], F32)
        mv = sb("mv", [P, NT, 2], F32)
        std = sb("std", [P, NT], F32)
        rstd = sb("rstd", [P, NT], F32)
        nmr = sb("nmr", [P, NT], F32)
        eps_t = sb("eps_t", [P, 1], F32)
        w_t = sb("w_t", [P, 2, C], F32)
        b_t = sb("b_t", [1, C], F32)
        b_rest = sb("b_rest", [1, C], F32)
        b_row = sb("b_row", [1, PARTS, C], BF16)
        b_parts = sb("b_parts", [PARTS, C], BF16)
        id_b = sb("id_b", [P, P], BF16)
        id_f = sb("id_f", [P, P], F32)
        tri_rank = sb("tri_rank", [P, P], BF16)
        tri_cut = sb("tri_cut", [P, P], BF16)
        ones_b = sb("ones_b", [P, P], BF16)
        count_w = sb("count_w", [P, NQ, NQ + 1], BF16)
        level_neg = sb("level_neg", [P, P], F32)
        one_t = sb("one_t", [P, 1], F32)
        off_by = sb("off_by", [P, 2, GN], BF16)
        chunk_f = sb("chunk_f", [1, NQ], F32)
        most = sb("most", [NQ + 1, 1], F32)
        counts = sb("counts", [1, NQ + 1], F32)
        extra = sb("extra", [1, NQ], F32)
        some = sb("some", [1, NQ], F32)
        keys = sb("keys", [1, NQ], F32)
        KEYS, ACTIVE, LONG = 0, NQ, NQ + 1
        more = sb("more", [1, 2, 16], I32)

        got = [pb(f"got{n}", [P, PAIR, GN], F32) for n in range(NP)]
        got_more = pb("got_more", [P, GN], F32)
        flip = pb("flip", [P, GN], BF16)
        prefix = pb("prefix", [P, GN], F32)
        misc = pb("misc", [P, GN], F32)

        adj_in = [sem("adj_in0"), sem("adj_in1")]
        x_in = sem("x_in")
        w_in = sem("w_in")
        b_in = sem("b_in")
        zeroed = sem("zeroed")
        consts = sem("consts")
        b_split = sem("b_split")
        abs_done = sem("abs_done")
        flip_done = sem("flip_done")
        mask_done = sem("mask_done")
        prefix_done = sem("prefix_done")
        rank_done = sem("rank_done")
        pick_done = sem("pick_done")
        got_done = sem("got_done")
        max_done = sem("max_done")
        off_done = sem("off_done")
        sel_done = sem("sel_done")
        more_got = sem("more_got")
        more_max = sem("more_max")
        joined = sem("joined")
        agg_done = sem("agg_done")
        count_done = sem("count_done")
        most_done = sem("most_done")
        most_row = sem("most_row")
        counts_done = sem("counts_done")
        key_step = sem("key_step")
        more_done = sem("more_done")
        cut_prefix = sem("cut_prefix")
        cut_mask = sem("cut_mask")
        hT_psum = sem("hT_psum")
        hT_done = sem("hT_done")
        fin_done = sem("fin_done")
        y_done = sem("y_done")
        out_st = [sem("out_st0"), sem("out_st1")]
        ln = sem("ln")
        std_done = sem("std_done")
        h_done = sem("h_done")
        split_act = sem("split_act")
        split_pool = sem("split_pool")
        passed = sem("passed")
        LN_OPS = 2 * NT + 2
        KEY_OPS = 5
        CONSTS = 8

        block = ctx.enter_context(nc.Block())

        def wait(eng, s, v):
            if v > 0:
                eng.wait_ge(s, v)

        def wait_apart(eng, s, v):
            eng.wait_ge(s, v)
            eng.sem_inc(passed, 1)

        def further_items(eng, par, item):
            active = eng.value_load(more[0:1, par, ACTIVE:ACTIVE + 1], min_val=0, max_val=NQ)
            with eng.If(active):
                with eng.Fori(0, active) as t:
                    key = eng.value_load(more[0:1, par, bass.ds(t, 1)], min_val=0, max_val=NQ * (P - STATIC) + NQ - 1)
                    with eng.Fori(0, key // NQ) as level:
                        item(key % NQ, level)
                eng.nop()

        @block.sync
        def _(sp):
            def load_adj(g):
                wait(sp, abs_done, NT * (g - 1))
                sp.dma_start(adj_i[:, g % 2, :, :], adj_g[:, g, :, :]).then_inc(adj_in[g % 2], 16)

            def load_x(g):
                sp.wait_ge(x_in, 16 * (g - 3))
                wait(sp, y_done, g - XB + 1)
                sp.dma_start(xs[:, g % XB, :, :], x_g[:, g, :, :]).then_inc(x_in, 16)

            sp.dma_start(xs[:, 0:4, :, :], x_g[:, 0:4, :, :]).then_inc(x_in, 16)
            for g in (0, 1):
                load_adj(g)
            sp.dma_start(w_t[:, :, :], w.rearrange("(two p) o -> p two o", p=P)).then_inc(w_in, 16)
            sp.dma_start(b_t[0:1, :], b.rearrange("(one o) -> one o", one=1)).then_inc(w_in, 16)
            for g in (2, 3):
                load_adj(g)
            sp.wait_ge(b_split, 5)
            for n in range(PARTS):
                sp.dma_start(b_parts[n:n + 1, :], b_row[0:1, n, :]).then_inc(b_in, 16)
            for k in range(G):
                if k + 4 < G:
                    load_adj(k + 4)
                    load_x(k + 4)
                sp.wait_ge(y_done, k + 1)
                sp.dma_start(out_g[:, k, :, :], y[:, k % 2, :, :]).then_inc(out_st[k % 2], 16)
            for par in (0, 1):
                sp.wait_ge(out_st[par], 8 * G)

        @block.gpsimd
        def _(pool):
            g_ = nc.gpsimd
            for t in (id_b, tri_rank, tri_cut, id_f, count_w):
                g_.memset(t[:], 0.0).then_inc(zeroed, 1)
            pool.wait_ge(zeroed, 5)
            for t, v in ((id_b, 1.0), (tri_rank, MARK), (tri_cut, CUT), (id_f, 1.0)):
                g_.affine_select(out=t[:], in_=t[:], compare_op=ALU.not_equal, fill=v, base=0,
                                 pattern=[[-1, P]], channel_multiplier=1).then_inc(zeroed, 1)
            for q in range(NQ):
                g_.memset(count_w[:, q, q:q + 1], 1.0)
                last = g_.memset(count_w[:, q, NQ:NQ + 1], 1.0)
            last.then_inc(consts, 1)
            pool.wait_ge(zeroed, 9)
            for t in (tri_rank, tri_cut):
                g_.affine_select(out=t[:], in_=t[:], compare_op=ALU.is_ge, fill=1.0, base=0,
                                 pattern=[[-1, P]], channel_multiplier=1).then_inc(consts, 1)
            g_.memset(ones_b[:], 1.0).then_inc(consts, 1)
            g_.memset(eps_t[:], EPS).then_inc(consts, 1)
            g_.memset(one_t[:], 1.0).then_inc(consts, 1)
            g_.iota(level_neg[:], pattern=[[-1, P]], base=-int(MARK), channel_multiplier=0,
                    allow_small_or_imprecise_dtypes=True).then_inc(consts, 1)
            g_.iota(chunk_f[:], pattern=[[1, NQ]], base=0, channel_multiplier=0,
                    allow_small_or_imprecise_dtypes=True).then_inc(consts, 1)
            pool.wait_ge(w_in, 32)
            g_.tensor_copy(b_row[0:1, 0, :], b_t[:]).then_inc(b_split, 1)
            pool.wait_ge(b_split, 1)
            g_.tensor_tensor(b_rest[:], b_t[:], b_row[0:1, 0, :], ALU.subtract).then_inc(b_split, 1)
            pool.wait_ge(b_split, 2)
            g_.tensor_copy(b_row[0:1, 1, :], b_rest[:]).then_inc(b_split, 1)
            pool.wait_ge(b_split, 3)
            g_.tensor_tensor(b_t[:], b_rest[:], b_row[0:1, 1, :], ALU.subtract).then_inc(b_split, 1)
            pool.wait_ge(b_split, 4)
            g_.tensor_copy(b_row[0:1, 2, :], b_t[:]).then_inc(b_split, 1)

            def part_of(g, n):
                return hpart[:, (g // 2) % 2, HQ * (g % 2):HQ * (g % 2 + 1), n, :]

            def rest_of_h(g):
                pool.wait_ge(split_act, 2 * g + 1)
                wait(pool, split_pool, 2 * g)
                g_.tensor_tensor(hrest[:], h32[:, g % 2, :, :], part_of(g, 0), ALU.subtract).then_inc(split_pool, 1)

            def third_part(g):
                pool.wait_ge(split_act, 2 * g + 2)
                g_.tensor_tensor(part_of(g, 2), hrest[:], part_of(g, 1), ALU.subtract).then_inc(split_pool, 1)

            def make_keys(g):
                m = more[0:1, g % 2, :]
                pool.wait_ge(counts_done, g + 1)
                wait(pool, agg_done, g - 1)
                g_.tensor_scalar(extra[:], counts[:, 0:NQ], float(-STATIC), 0.0, ALU.add, ALU.max).then_inc(key_step, 1)
                g_.tensor_scalar(m[:, LONG:LONG + 1], counts[:, NQ:NQ + 1], float(-KEEP), 0.0, ALU.add, ALU.max).then_inc(key_step, 1)
                pool.wait_ge(key_step, KEY_OPS * g + 1)
                g_.tensor_scalar(some[:], extra[:], 1.0, None, ALU.min).then_inc(key_step, 1)
                wait(pool, more_done, g)
                g_.tensor_scalar(keys[:], extra[:], float(NQ), None, ALU.mult).then_inc(key_step, 1)
                pool.wait_ge(key_step, KEY_OPS * g + 4)
                g_.tensor_tensor(keys[:], keys[:], chunk_f[:], ALU.add).then_inc(key_step, 1)

            for g in (0, 1):
                rest_of_h(g)
                third_part(g)
                if g == 0:
                    make_keys(0)
            for k in range(G):
                if 0 < k < G - 1:
                    third_part(k + 1)
                if k + 1 < G:
                    make_keys(k + 1)
                if k + 2 < G:
                    rest_of_h(k + 2)

        @block.scalar
        def _(act):
            def absolute(g, t):
                act.wait_ge(adj_in[g % 2], 16 * (g // 2 + 1))
                wait(act, flip_done, NQ * (g - 1))
                nc.scalar.activation(adj_a[:, g % 2, t, :], adj_i[:, g % 2, t, :], ACT.Abs).then_inc(abs_done, 1)

            def mask(g, q):
                act.wait_ge(flip_done, NQ * g + q + 1)
                wait(act, prefix_done, NQ * (g - 1))
                nc.scalar.activation(maskT[:, g % 2, q, :], flip[:], ACT.Sign).then_inc(mask_done, 1)

            def ranks(g, q):
                act.wait_ge(prefix_done, NQ * g + q + 1)
                wait(act, pick_done, STATIC * 2 * (g - 1))
                wait(act, agg_done, g - 1)
                nc.scalar.copy(rank[:, g % 2, q, :], prefix[:]).then_inc(rank_done, 1)

            def deviation(g):
                act.wait_ge(ln, LN_OPS * g + 2 * NT)
                nc.scalar.activation(std[:], mv[:, :, 1], ACT.Sqrt, bias=eps_t[:, 0:1]).then_inc(std_done, 1)

            def normalise(g):
                act.wait_ge(ln, LN_OPS * (g + 1))
                wait(act, hT_psum, g - 1)
                for t in range(NT):
                    nc.scalar.activation(h32[:, g % 2, t, :], xs[:, g % XB, t, :], ACT.Relu,
                                         bias=nmr[:, t:t + 1], scale=rstd[:, t:t + 1]).then_inc(h_done, 1)

            def part_of(g, n):
                return hpart[:, (g // 2) % 2, HQ * (g % 2):HQ * (g % 2 + 1), n, :]

            def first_part(g):
                act.wait_ge(h_done, NT * (g + 1))
                wait(act, agg_done, g - 2)
                nc.scalar.copy(part_of(g, 0), h32[:, g % 2, :, :]).then_inc(split_act, 1)

            def second_part(g):
                act.wait_ge(split_pool, 2 * g + 1)
                nc.scalar.copy(part_of(g, 1), hrest[:]).then_inc(split_act, 1)

            def turned_h(g):
                act.wait_ge(hT_psum, g + 1)
                wait(act, fin_done, g - 1)
                nc.scalar.copy(hT[:, g % 2, :], misc[:]).then_inc(hT_done, 1)

            def row_of_counts(g):
                act.wait_ge(most_row, g + 1)
                wait(act, key_step, KEY_OPS * g)
                nc.scalar.copy(counts[:], misc[0:1, 0:NQ + 1]).then_inc(counts_done, 1)

            def select(g):
                act.wait_ge(more_done, g + 1)

                def item(chunk, level):
                    s = act.snap(sel, min_val=0, max_val=G * NQ * P)
                    wait_apart(act, sel_done, s + 1)
                    wait_apart(act, more_got, s + 1)
                    nc.scalar.activation(off_by[:, bass.ds(s % 2, 1), :], rank[:, g % 2, bass.ds(chunk, 1), :], ACT.Abs,
                                         bias=level_neg[:, bass.ds(level + STATIC, 1)]).then_inc(off_done, 1)
                    wait_apart(act, off_done, s + 1)
                    nc.scalar.activation(pick_more[:, bass.ds(s % SEL, 1), :], off_by[:, bass.ds(s % 2, 1), :], ACT.Relu,
                                         bias=one_t[:, 0:1], scale=-1.0).then_inc(sel_done, 1)
                    act.reg_add(sel, sel, 1)

                further_items(act, g % 2, item)

            sel = act.alloc_register("act_sel")
            act.reg_mov(sel, 0)
            act.sem_inc(sel_done, 2)
            act.wait_ge(consts, CONSTS)
            for t in range(NT):
                absolute(0, t)
            deviation(0)
            normalise(0)
            first_part(0)
            for q in range(NQ):
                mask(0, q)
                if q == 2:
                    second_part(0)
                if q < NT:
                    absolute(1, q)
            row_of_counts(0)
            deviation(1)
            normalise(1)
            first_part(1)
            for q in range(NQ):
                ranks(0, q)
                mask(1, q)
                if q == 2:
                    second_part(1)
                if q < NT:
                    absolute(2, q)

            for k in range(G):
                for q in range(NQ):
                    if q >= HQ and k + 1 < G:
                        ranks(k + 1, 2 * q - NQ)
                    if q == HQ:
                        select(k)
                    if q == 5 and k + 2 < G:
                        deviation(k + 2)
                    if k + 2 < G:
                        mask(k + 2, q)
                    if q < NT and k + 3 < G:
                        absolute(k + 3, q)
                    if q >= HQ and k + 1 < G:
                        ranks(k + 1, 2 * q - NQ + 1)
                    if q == 0 and 0 < k < G - 1:
                        second_part(k + 1)
                    if q == 1 and k + 1 < G:
                        row_of_counts(k + 1)
                    if q == 3:
                        turned_h(k)
                    if q == 6 and k + 2 < G:
                        normalise(k + 2)
                        first_part(k + 2)

        @block.tensor
        def _(pe):
            pe.sem_inc(more_got, SEL)
            further = pe.alloc_register("pe_further")
            pe.reg_mov(further, 0)
            cuts = pe.alloc_register("pe_cuts")
            pe.reg_mov(cuts, 0)

            def transpose(g, q):
                pe.wait_ge(abs_done, NT * (g + 1))
                wait(pe, mask_done, NQ * g + q)
                for t in range(NT):
                    last = nc.tensor.transpose(flip[:, t * P:(t + 1) * P], adj_a[:, g % 2, t, q * P:(q + 1) * P], id_b[:])
                last.then_inc(flip_done, 1)

            def number(g, q):
                pe.wait_ge(mask_done, NQ * g + q + 1)
                wait(pe, rank_done, NQ * g + q)
                nc.tensor.matmul(prefix[:], tri_rank[:], maskT[:, g % 2, q, :], start=True, stop=True).then_inc(prefix_done, 1)

            def count(g):
                pe.wait_ge(mask_done, NQ * (g + 1))
                wait(pe, hT_done, g - 1)
                for q in range(NQ):
                    last = nc.tensor.matmul(misc[0:NQ + 1, :], count_w[:, q, :], maskT[:, g % 2, q, :],
                                            start=(q == 0), stop=(q == NQ - 1))
                last.then_inc(count_done, 1)

            def count_row(g):
                pe.wait_ge(most_done, g + 1)
                nc.tensor.matmul(misc[0:1, 0:NQ + 1], most[:, 0:1], id_f[0:NQ + 1, 0:NQ + 1],
                                 start=True, stop=True).then_inc(most_row, 1)

            def cut(g):
                pe.wait_ge(more_done, g + 1)
                wait(pe, rank_done, NQ * g)
                with pe.If(pe.value_load(more[0:1, g % 2, LONG:LONG + 1], min_val=0, max_val=N)):
                    done = pe.snap(cuts, min_val=0, max_val=NQ * G)
                    for n, q in enumerate(range(NQ - 1, -1, -1)):
                        if n:
                            pe.wait_ge(cut_mask, done + n)
                        for before in range(q):
                            nc.tensor.matmul(prefix[:], ones_b[:], maskT[:, g % 2, before, :], start=(before == 0), stop=False)
                        nc.tensor.matmul(prefix[:], tri_cut[:], maskT[:, g % 2, q, :], start=(q == 0), stop=True).then_inc(cut_prefix, 1)
                    pe.wait_ge(cut_mask, done + NQ)
                    pe.reg_add(cuts, cuts, NQ)
                pe.nop()

            def gather(k, q):
                if q % HQ == 0:
                    pe.wait_ge(split_pool, 2 * (k - k % 2 + q // HQ + 1))
                for n in range(NP):
                    wait(pe, max_done, NP * (NQ * k + q - 1) + n + 1)
                    for i in range(PAIR):
                        j = PAIR * n + i
                        if q % HQ == 0:
                            pe.wait_ge(pick_done, STATIC * (2 * k + q // HQ) + j + 1)
                        for part in range(PARTS):
                            last = nc.tensor.matmul(got[n][:, i, :], hpart[:, (k // 2) % 2, q, part, :], pick[:, q // HQ, j, q % HQ, :],
                                                    start=(part == 0), stop=(part == PARTS - 1))
                    last.then_inc(got_done, 1)

            def gather_more(k):
                def item(chunk, level):
                    d = pe.snap(further, min_val=0, max_val=G * NQ * P)
                    pe.wait_ge(sel_done, d + 3)
                    pe.wait_ge(more_max, d + 1)
                    for part in range(PARTS):
                        last = nc.tensor.matmul(got_more[:], hpart[:, (k // 2) % 2, bass.ds(chunk, 1), part, :].rearrange("p o c -> p (o c)"),
                                                pick_more[:, bass.ds(d % SEL, 1), :], start=(part == 0), stop=(part == PARTS - 1))
                    last.then_inc(more_got, 1)
                    pe.reg_add(further, further, 1)

                further_items(pe, k % 2, item)

            def turn_h(g):
                pe.wait_ge(h_done, NT * (g + 1))
                wait(pe, y_done, g)
                pe.wait_ge(counts_done, min(g + 2, G))
                for t in range(NT):
                    last = nc.tensor.transpose(misc[:, t * P:(t + 1) * P], h32[:, g % 2, t, :], id_f[:])
                last.then_inc(hT_psum, 1)

            def finish(g):
                pe.wait_ge(agg_done, g + 1)
                pe.wait_ge(hT_done, min(g + 1, G))
                pe.wait_ge(counts_done, min(g + 3, G) if g + 1 < G else G)
                if g == 0:
                    pe.wait_ge(w_in, 32)
                    pe.wait_ge(b_in, 16 * PARTS)
                for t in range(NT):
                    o = misc[:, t * P:(t + 1) * P]
                    nc.tensor.matmul(o, hT[:, g % 2, t * P:(t + 1) * P], w_t[:, 0, :], start=True, stop=False)
                    nc.tensor.matmul(o, ones_b[0:PARTS, :], b_parts[:], start=False, stop=False)
                    last = nc.tensor.matmul(o, agg[:, g % 2, t * P:(t + 1) * P], w_t[:, 1, :], start=False, stop=True)
                last.then_inc(fin_done, 1)

            pe.wait_ge(consts, CONSTS)
            for q in range(NQ):
                transpose(0, q)
            count(0)
            count_row(0)
            cut(0)
            for q in range(NQ):
                number(0, q)
                transpose(1, q)

            for k in range(G):
                for q in range(NQ):
                    if q == HQ + 1:
                        gather_more(k)
                    if q >= HQ and k + 1 < G:
                        number(k + 1, 2 * q - NQ)
                    gather(k, q)
                    if k + 2 < G:
                        transpose(k + 2, q)
                    if q >= HQ and k + 1 < G:
                        number(k + 1, 2 * q - NQ + 1)
                    if q == 0 and k + 1 < G:
                        count(k + 1)
                    if q == 1 and k + 1 < G:
                        count_row(k + 1)
                    if q == 2 and k > 0:
                        finish(k - 1)
                    if q == 3:
                        turn_h(k)
                        if k + 1 < G:
                            cut(k + 1)
            finish(G - 1)

        @block.vector
        def _(dve):
            v = nc.vector
            dve.sem_inc(more_max, 1)
            further = dve.alloc_register("dve_further")
            dve.reg_mov(further, 0)
            cuts = dve.alloc_register("dve_cuts")
            dve.reg_mov(cuts, 0)

            def moments(g):
                dve.wait_ge(x_in, 16 * (max(g, 3) - 2))
                for t in range(NT):
                    v.bn_stats(stats[:, t, :], xs[:, g % XB, t, :]).then_inc(ln, 1)
                for t in range(NT):
                    dve.wait_ge(ln, LN_OPS * g + t + 1)
                    v.bn_aggr(mv[:, t, :], stats[:, t, :]).then_inc(ln, 1)

            def scale_bias(g):
                dve.wait_ge(std_done, g + 1)
                wait(dve, h_done, NT * g)
                v.reciprocal(rstd[:], std[:]).then_inc(ln, 1)
                dve.wait_ge(ln, LN_OPS * g + 2 * NT + 1)
                v.scalar_tensor_tensor(nmr[:], mv[:, :, 0], -1.0, rstd[:], ALU.mult, ALU.mult).then_inc(ln, 1)

            def picks(g, half):
                dve.wait_ge(rank_done, NQ * g + HQ * (half + 1))
                wait(dve, got_done, NP * (NQ * (g - 1) + HQ * (half + 1)))
                for j in range(STATIC):
                    v.tensor_scalar(pick[:, half, j, :, :], rank[:, g % 2, HQ * half:HQ * (half + 1), :], MARK + j, None,
                                    ALU.is_equal).then_inc(pick_done, 1)

            def most_of(g):
                dve.wait_ge(count_done, g + 1)
                v.reduce_max(most[:, 0:1], misc[0:NQ + 1, :], AX.X).then_inc(most_done, 1)

            def sort_keys(g):
                dve.wait_ge(key_step, KEY_OPS * (g + 1))
                with nc.allow_low_precision(reason="a sum of NQ values 0 or 1"):
                    v.reduce_sum(more[0:1, g % 2, ACTIVE:ACTIVE + 1], some[:], AX.X)
                v.max(more[0:1, g % 2, KEYS:KEYS + NQ], keys[:]).then_inc(more_done, 1)

            def cut(g):
                dve.wait_ge(more_done, g + 1)
                with dve.If(dve.value_load(more[0:1, g % 2, LONG:LONG + 1], min_val=0, max_val=N)):
                    done = dve.snap(cuts, min_val=0, max_val=NQ * G)
                    for n, q in enumerate(range(NQ - 1, -1, -1)):
                        dve.wait_ge(cut_prefix, done + n + 1)
                        v.tensor_scalar(maskT[:, g % 2, q, :], prefix[:], CUT + KEEP - 1, None, ALU.is_le).then_inc(cut_mask, 1)
                    dve.reg_add(cuts, cuts, NQ)
                dve.nop()

            def maxima(k, q):
                for n in range(NP):
                    pair = NP * (NQ * k + q) + n
                    dve.wait_ge(got_done, pair + 1)
                    if q == 0:
                        wait(dve, agg_done, k)
                        v.tensor_scalar(acc[:, n, :, :], got[n][:], 0.0, None, ALU.max).then_inc(max_done, 1)
                    else:
                        dve.wait_ge(max_done, pair + 1 - NP)
                        v.tensor_tensor(acc[:, n, :, :], acc[:, n, :, :], got[n][:], ALU.max).then_inc(max_done, 1)

            def maxima_more(k, q):
                dve.wait_ge(max_done, NP * (NQ * k + q + 1))

                def item(chunk, level):
                    d = dve.snap(further, min_val=0, max_val=G * NQ * P)
                    dve.wait_ge(more_got, d + 1 + SEL)
                    dve.wait_ge(more_max, d + 1)
                    v.tensor_tensor(acc[:, 0, 0, :], acc[:, 0, 0, :], got_more[:], ALU.max).then_inc(more_max, 1)
                    dve.reg_add(further, further, 1)

                further_items(dve, k % 2, item)
                dve.wait_ge(more_max, dve.snap(further, min_val=0, max_val=G * NQ * P) + 1)

            def join(k):
                dve.wait_ge(max_done, NP * NQ * (k + 1))
                v.tensor_tensor(acc[:, 0, :, :], acc[:, 0, :, :], acc[:, 1, :, :], ALU.max).then_inc(joined, 1)
                dve.wait_ge(joined, k + 1)
                v.tensor_tensor(agg[:, k % 2, :], acc[:, 0, 0, :], acc[:, 0, 1, :], ALU.max).then_inc(agg_done, 1)

            def output(g):
                dve.wait_ge(fin_done, g + 1)
                wait(dve, out_st[g % 2], 16 * (g // 2))
                v.scalar_tensor_tensor(y[:, g % 2, :, :], misc[:].rearrange("p (t c) -> p t c", t=NT), 0.0,
                                       xs[:, g % XB, :, :], ALU.max, ALU.add).then_inc(y_done, 1)

            for g in (0, 1):
                moments(g)
                scale_bias(g)
                if g == 0:
                    most_of(0)
                    sort_keys(0)
                    cut(0)
            picks(0, 0)
            for k in range(G):
                for q in range(NQ):
                    if q == HQ + 1:
                        maxima_more(k, q - 1)
                    maxima(k, q)
                    if q == 0 and k + 1 < G:
                        most_of(k + 1)
                    if q == 1:
                        picks(k, 1)
                    if q == 2 and k + 1 < G:
                        sort_keys(k + 1)
                    if q == 2 and k > 0:
                        output(k - 1)
                    if q == 3 and k + 1 < G:
                        cut(k + 1)
                    if q == 4 and k + 2 < G:
                        moments(k + 2)
                    if q == 6 and k + 2 < G:
                        scale_bias(k + 2)
                    if q == 6 and k + 1 < G:
                        picks(k + 1, 0)
                join(k)
            output(G - 1)


_INS = ['x', 'adj', 'L0_gnn_W', 'L0_gnn_b']
_OUTS = [((8, 1024, 128), 'float32')]


def kernel(**inputs):
    import numpy as _np
    import concourse.bacc as _bacc
    from concourse import mybir as _mybir
    from concourse.bass_utils import run_bass_kernel_spmd as _run

    nc = _bacc.Bacc("TRN2", target_bir_lowering=False, num_devices=1)
    arrays, args = {}, []
    for name in _INS:
        a = _np.ascontiguousarray(inputs[name])
        arrays[f"in_{name}_dram"] = a
        args.append(nc.dram_tensor(f"in_{name}_dram", a.shape, _mybir.dt.from_np(a.dtype), kind="ExternalInput").ap())
    for i, (shape, dtype) in enumerate(_OUTS):
        dt = _mybir.dt.from_np(_np.dtype(dtype))
        args.append(nc.dram_tensor(f"out_{i}_dram", shape, dt, kind="ExternalOutput").ap())
    gnn_layer(nc, *args)
    r = _run(nc, [arrays], core_ids=[0])
    got = tuple(r.results[0][f"out_{i}_dram"] for i in range(len(_OUTS)))
    return got[0]
```

```python
import concourse.bass as bass
from concourse import mybir
from contextlib import ExitStack

F32 = mybir.dt.float32
BF16 = mybir.dt.bfloat16
I32 = mybir.dt.int32
ALU = mybir.AluOpType
ACT = mybir.ActivationFunctionType
AX = mybir.AxisListType

P = 128
EPS = 1e-5
KEEP = 25
STATIC = 4
PAIR = 2
MARK = 128.0
CUT = -4096.0
SEL = 4
PARTS = 3


def gnn_layer(nc, x, adj, w, b, out):
    B, N, C = x.shape
    NQ = N // P
    NT = 4
    GN = NT * P
    HQ = NQ // 2
    G = B * N // GN
    NP = STATIC // PAIR
    XB = 8

    adj_g = adj.rearrange("b (g t p) m -> p (b g) t m", t=NT, p=P)
    x_g = x.rearrange("b (g t p) c -> p (b g) t c", t=NT, p=P)
    out_g = out.rearrange("b (g t p) c -> p (b g) t c", t=NT, p=P)

    ctx = ExitStack()
    with ctx:
        def sb(name, shape, dt):
            return ctx.enter_context(nc.sbuf_tensor(name, shape, dt))

        def pb(name, shape, dt):
            return ctx.enter_context(nc.psum_tensor(name, shape, dt))

        def sem(name):
            return ctx.enter_context(nc.semaphore(name))

        adj_i = sb("adj_i", [P, 2, NT, N], I32)
        adj_a = sb("adj_a", [P, 2, NT, N], BF16)
        maskT = sb("maskT", [P, 2, NQ, GN], BF16)
        rank = sb("rank", [P, 2, NQ, GN], BF16)
        pick = sb("pick", [P, 2, STATIC, HQ, GN], BF16)
        pick_more = sb("pick_more", [P, SEL, GN], BF16)
        xs = sb("xs", [P, XB, NT, C], F32)
        h32 = sb("h32", [P, 2, NT, C], F32)
        hpart = sb("hpart", [P, 2, NQ, PARTS, C], BF16)
        hrest = sb("hrest", [P, NT, C], F32)
        hT = sb("hT", [P, 2, GN], F32)
        acc = sb("acc", [P, 2, NP, PAIR, GN], F32)
        agg = sb("agg", [P, 2, GN], F32)
        y = sb("y", [P, 2, NT, C], F32)
        stats = sb("stats", [P, NT, 6], F32)
        mv = sb("mv", [P, NT, 2], F32)
        std = sb("std", [P, NT], F32)
        rstd = sb("rstd", [P, NT], F32)
        nmr = sb("nmr", [P, NT], F32)
        eps_t = sb("eps_t", [P, 1], F32)
        w_t = sb("w_t", [P, 2, C], F32)
        b_t = sb("b_t", [1, C], F32)
        b_rest = sb("b_rest", [1, C], F32)
        b_row = sb("b_row", [1, PARTS, C], BF16)
        b_parts = sb("b_parts", [PARTS, C], BF16)
        id_b = sb("id_b", [P, P], BF16)
        id_f = sb("id_f", [P, P], F32)
        tri_rank = sb("tri_rank", [P, P], BF16)
        tri_cut = sb("tri_cut", [P, P], BF16)
        ones_b = sb("ones_b", [P, P], BF16)
        level_neg = sb("level_neg", [P, P], F32)
        one_t = sb("one_t", [P, 1], F32)
        off_by = sb("off_by", [P, 2, GN], BF16)
        chunk_f = sb("chunk_f", [1, NQ], F32)
        degree = sb("degree", [P, 4, NT], F32)
        degree_most = sb("degree_most", [P, 1], F32)
        excess = sb("excess", [1, P], F32)
        excess_sum = sb("excess_sum", [1, 1], F32)
        keep_neg = sb("keep_neg", [P, 1], F32)
        long_i = sb("long_i", [1, 2], I32)
        last_row = sb("last_row", [NQ * NT, P], BF16)
        above = sb("above", [NQ * NT, P], BF16)
        in_chunk = sb("in_chunk", [NQ * NT, P], BF16)
        most = sb("most", [NQ * NT, 1], F32)
        counts = sb("counts", [1, NQ], F32)
        extra = sb("extra", [1, NQ], F32)
        some = sb("some", [1, NQ], F32)
        keys = sb("keys", [1, NQ], F32)
        KEYS, ACTIVE, TOTAL = 0, NQ, NQ + 1
        more = sb("more", [1, 2, 16], I32)

        got = [pb(f"got{n}", [P, PAIR, GN], F32) for n in range(NP)]
        got_more = pb("got_more", [P, GN], F32)
        flip = pb("flip", [P, GN], BF16)
        prefix = pb("prefix", [P, GN], F32)
        misc = pb("misc", [P, GN], F32)
        flip_odd = got[1][:, 0, :].bitcast(BF16)[:, 0:GN]
        prefix_odd = got[1][:, 1, :]

        adj_in = [sem("adj_in0"), sem("adj_in1")]
        adj_first = [sem(f"adj_first{t}") for t in range(NT)]
        x_first = sem("x_first")
        x_in = sem("x_in")
        w_in = sem("w_in")
        b_in = sem("b_in")
        zeroed = sem("zeroed")
        consts = sem("consts")
        b_split = sem("b_split")
        abs_done = sem("abs_done")
        flip_done = sem("flip_done")
        mask_done = sem("mask_done")
        mask_dve = sem("mask_dve")
        prefix_done = sem("prefix_done")
        rank_done = sem("rank_done")
        rank_dve = sem("rank_dve")
        pick_done = sem("pick_done")
        got_done = sem("got_done")
        started = sem("started")
        max_done = sem("max_done")
        off_done = sem("off_done")
        sel_done = sem("sel_done")
        more_got = sem("more_got")
        more_max = sem("more_max")
        joined = sem("joined")
        agg_done = sem("agg_done")
        tile_most = sem("tile_most")
        degree_row = sem("degree_row")
        degree_read = sem("degree_read")
        long_done = sem("long_done")
        rows_in = sem("rows_in")
        counting = sem("counting")
        most_done = sem("most_done")
        most_row = sem("most_row")
        counts_done = sem("counts_done")
        key_step = sem("key_step")
        more_done = sem("more_done")
        cut_prefix = sem("cut_prefix")
        cut_mask = sem("cut_mask")
        hT_psum = sem("hT_psum")
        hT_done = sem("hT_done")
        fin_done = sem("fin_done")
        relu_done = sem("relu_done")
        y_done = sem("y_done")
        out_st = [sem("out_st0"), sem("out_st1")]
        ln = sem("ln")
        std_done = sem("std_done")
        h_done = sem("h_done")
        split_act = sem("split_act")
        split_pool = sem("split_pool")
        passed = sem("passed")
        LN_OPS = 2 * NT + 2
        KEY_OPS = 4
        CONSTS = 8

        block = ctx.enter_context(nc.Block())

        def wait(eng, s, v):
            if v > 0:
                eng.wait_ge(s, v)

        def wait_masks(eng, g):
            eng.wait_ge(mask_done, NQ * (g + 1))
            eng.wait_ge(mask_dve, HQ * min(g + 1, 2))

        def wait_taken(eng, k, q, n):
            if q == 0:
                eng.wait_ge(started, NP * k + n + 1)
            else:
                eng.wait_ge(max_done, NP * ((NQ - 1) * k + q - 1) + n + 1)

        def wait_apart(eng, s, v):
            eng.wait_ge(s, v)
            eng.sem_inc(passed, 1)

        def chunks_with_more(eng, par):
            return eng.value_load(more[0:1, par, ACTIVE:ACTIVE + 1], min_val=0, max_val=NQ)

        def further_items(eng, par, active, item):
            with eng.If(active):
                with eng.Fori(0, active) as t:
                    key = eng.value_load(more[0:1, par, bass.ds(t, 1)], min_val=0, max_val=NQ * (P - STATIC) + NQ - 1)
                    with eng.Fori(0, key // NQ) as level:
                        item(key % NQ, level)
                eng.nop()

        @block.sync
        def _(sp):
            def load_adj(g):
                wait(sp, abs_done, NT * (g - 1))
                sp.dma_start(adj_i[:, g % 2, :, :], adj_g[:, g, :, :]).then_inc(adj_in[g % 2], 16)

            def load_x(g):
                sp.wait_ge(x_in, 16 * (g - 3))
                wait(sp, y_done, g - XB + 1)
                sp.dma_start(xs[:, g % XB, :, :], x_g[:, g, :, :]).then_inc(x_in, 16)

            sp.dma_start(xs[:, 0, :, :], x_g[:, 0, :, :]).then_inc(x_first, 16)
            for t in range(NT):
                sp.dma_start(adj_i[:, 0, t, :], adj_g[:, 0, t, :]).then_inc(adj_first[t], 16)
            sp.dma_start(xs[:, 1:4, :, :], x_g[:, 1:4, :, :]).then_inc(x_in, 16)
            load_adj(1)
            sp.dma_start(w_t[:, :, :], w.rearrange("(two p) o -> p two o", p=P)).then_inc(w_in, 16)
            sp.dma_start(b_t[0:1, :], b.rearrange("(one o) -> one o", one=1)).then_inc(w_in, 16)
            for g in (2, 3):
                load_adj(g)

            def load_rows(g):
                sp.wait_ge(rank_done, NQ * (g + 1))
                sp.wait_ge(rank_dve, HQ)
                wait(sp, most_done, g)
                sp.dma_start(last_row[:], rank[P - 1:P, g % 2, :, :].rearrange("o q (t n) -> o (q t) n", t=NT)).then_inc(rows_in, 16)

            load_rows(0)
            for k in range(G):
                if k + 4 < G:
                    load_adj(k + 4)
                    load_x(k + 4)
                if k + 1 < G:
                    load_rows(k + 1)
                if k == 0:
                    sp.wait_ge(b_split, 5)
                    for n in range(PARTS):
                        sp.dma_start(b_parts[n:n + 1, :], b_row[0:1, n, :]).then_inc(b_in, 16)
                sp.wait_ge(y_done, k + 1)
                sp.dma_start(out_g[:, k, :, :], y[:, k % 2, :, :]).then_inc(out_st[k % 2], 16)
            for par in (0, 1):
                sp.wait_ge(out_st[par], 8 * G)

        @block.gpsimd
        def _(pool):
            g_ = nc.gpsimd
            for t in (id_b, tri_rank, tri_cut, id_f):
                g_.memset(t[:], 0.0).then_inc(zeroed, 1)
            pool.wait_ge(zeroed, 4)
            for t, v in ((id_b, 1.0), (tri_rank, MARK), (tri_cut, CUT), (id_f, 1.0)):
                g_.affine_select(out=t[:], in_=t[:], compare_op=ALU.not_equal, fill=v, base=0,
                                 pattern=[[-1, P]], channel_multiplier=1).then_inc(zeroed, 1)
            pool.wait_ge(zeroed, 8)
            for t in (tri_rank, tri_cut):
                g_.affine_select(out=t[:], in_=t[:], compare_op=ALU.is_ge, fill=1.0, base=0,
                                 pattern=[[-1, P]], channel_multiplier=1).then_inc(consts, 1)
            g_.memset(ones_b[:], 1.0).then_inc(consts, 1)
            g_.memset(eps_t[:], EPS).then_inc(consts, 1)
            g_.memset(one_t[:], 1.0).then_inc(consts, 1)
            g_.memset(keep_neg[:], -float(KEEP)).then_inc(consts, 1)
            g_.iota(level_neg[:], pattern=[[-1, P]], base=-int(MARK), channel_multiplier=0,
                    allow_small_or_imprecise_dtypes=True).then_inc(consts, 1)
            g_.iota(chunk_f[:], pattern=[[1, NQ]], base=0, channel_multiplier=0,
                    allow_small_or_imprecise_dtypes=True).then_inc(consts, 1)
            def part_of(g, n):
                return hpart[:, (g // 2) % 2, HQ * (g % 2):HQ * (g % 2 + 1), n, :]

            def rest_of_h(g):
                pool.wait_ge(split_act, 2 * g + 1)
                wait(pool, split_pool, 2 * g)
                g_.tensor_tensor(hrest[:], h32[:, g % 2, :, :], part_of(g, 0), ALU.subtract).then_inc(split_pool, 1)

            def third_part(g):
                pool.wait_ge(split_act, 2 * g + 2)
                g_.tensor_tensor(part_of(g, 2), hrest[:], part_of(g, 1), ALU.subtract).then_inc(split_pool, 1)

            def split_b():
                pool.wait_ge(w_in, 32)
                g_.tensor_copy(b_row[0:1, 0, :], b_t[:]).then_inc(b_split, 1)
                pool.wait_ge(b_split, 1)
                g_.tensor_tensor(b_rest[:], b_t[:], b_row[0:1, 0, :], ALU.subtract).then_inc(b_split, 1)
                pool.wait_ge(b_split, 2)
                g_.tensor_copy(b_row[0:1, 1, :], b_rest[:]).then_inc(b_split, 1)
                pool.wait_ge(b_split, 3)
                g_.tensor_tensor(b_t[:], b_rest[:], b_row[0:1, 1, :], ALU.subtract).then_inc(b_split, 1)
                pool.wait_ge(b_split, 4)
                g_.tensor_copy(b_row[0:1, 2, :], b_t[:]).then_inc(b_split, 1)

            def count_chunks(g):
                pool.wait_ge(rows_in, 16 * (g + 1))
                wait(pool, most_done, g)
                g_.tensor_scalar(above[:], last_row[:], MARK, 1.0 - MARK, ALU.is_ge, ALU.mult).then_inc(counting, 1)
                pool.wait_ge(counting, 2 * g + 1)
                g_.tensor_tensor(in_chunk[:], last_row[:], above[:], ALU.add).then_inc(counting, 1)

            def add_x(g):
                pool.wait_ge(relu_done, g + 1)
                g_.tensor_tensor(y[:, g % 2, :, :], y[:, g % 2, :, :], xs[:, g % XB, :, :], ALU.add).then_inc(y_done, 1)

            def make_keys(g):
                pool.wait_ge(counts_done, g + 1)
                wait(pool, agg_done, g - 1)
                g_.tensor_scalar(extra[:], counts[:, 0:NQ], float(-STATIC), 0.0, ALU.add, ALU.max).then_inc(key_step, 1)
                pool.wait_ge(key_step, KEY_OPS * g + 1)
                g_.tensor_scalar(some[:], extra[:], 1.0, None, ALU.min).then_inc(key_step, 1)
                wait(pool, more_done, g)
                g_.tensor_scalar(keys[:], extra[:], float(NQ), None, ALU.mult).then_inc(key_step, 1)
                pool.wait_ge(key_step, KEY_OPS * g + 3)
                g_.tensor_tensor(keys[:], keys[:], chunk_f[:], ALU.add).then_inc(key_step, 1)

            for g in (0, 1):
                rest_of_h(g)
                third_part(g)
            for k in range(G):
                count_chunks(k)
                if 0 < k < G - 1:
                    rest_of_h(k + 1)
                    third_part(k + 1)
                make_keys(k)
                if k == 0:
                    split_b()
                if k > 0:
                    add_x(k - 1)
            add_x(G - 1)

        @block.scalar
        def _(act):
            def absolute(g, t):
                if g == 0:
                    act.wait_ge(adj_first[t], 16)
                else:
                    act.wait_ge(adj_in[g % 2], 16 * ((g + 1) // 2))
                wait(act, flip_done, NQ * (g - 1))
                wait(act, tile_most, g - 3)
                nc.scalar.activation(adj_a[:, g % 2, t, :], adj_i[:, g % 2, t, :], ACT.Abs,
                                     accum_out=degree[:, g % 4, t:t + 1]).then_inc(abs_done, 1)

            def mask(g, q, counted=1):
                act.wait_ge(flip_done, NQ * g + q + 1)
                wait(act, prefix_done, NQ * (g - 1))
                nc.scalar.activation(maskT[:, g % 2, q, :], flip[:], ACT.Sign).then_inc(mask_done, counted)

            def ranks(g, q, counted=1):
                act.wait_ge(prefix_done, NQ * g + q + 1)
                wait(act, pick_done, STATIC * 2 * (g - 1))
                wait(act, agg_done, g - 1)
                nc.scalar.copy(rank[:, g % 2, q, :], prefix[:]).then_inc(rank_done, counted)

            def deviation(g):
                act.wait_ge(ln, LN_OPS * g + 2 * NT)
                nc.scalar.activation(std[:], mv[:, :, 1], ACT.Sqrt, bias=eps_t[:, 0:1]).then_inc(std_done, 1)

            def normalise(g, tiles=range(NT)):
                act.wait_ge(ln, LN_OPS * (g + 1))
                wait(act, hT_psum, g - 1)
                for t in tiles:
                    nc.scalar.activation(h32[:, g % 2, t, :], xs[:, g % XB, t, :], ACT.Relu,
                                         bias=nmr[:, t:t + 1], scale=rstd[:, t:t + 1]).then_inc(h_done, 1)

            def part_of(g, n):
                return hpart[:, (g // 2) % 2, HQ * (g % 2):HQ * (g % 2 + 1), n, :]

            def first_part(g):
                act.wait_ge(h_done, NT * (g + 1))
                wait(act, agg_done, g - 2)
                nc.scalar.copy(part_of(g, 0), h32[:, g % 2, :, :]).then_inc(split_act, 1)

            def second_part(g):
                act.wait_ge(split_pool, 2 * g + 1)
                nc.scalar.copy(part_of(g, 1), hrest[:]).then_inc(split_act, 1)

            def start_maxima(k, n):
                act.wait_ge(got_done, NP * NQ * k + n + 1)
                wait(act, agg_done, k - 1)
                nc.scalar.copy(acc[:, k % 2, n, :, :], got[n][:]).then_inc(started, 1)

            def turned_h(g):
                act.wait_ge(hT_psum, g + 1)
                wait(act, fin_done, g - 1)
                nc.scalar.copy(hT[:, g % 2, :], misc[:]).then_inc(hT_done, 1)

            def is_long(g):
                act.wait_ge(degree_row, g + 1)
                wait(act, long_done, g)
                nc.scalar.activation(excess[:], misc[0:1, 0:P], ACT.Relu, bias=keep_neg[0:1, 0:1],
                                     accum_out=excess_sum[:]).then_inc(degree_read, 1)
                act.wait_ge(degree_read, g + 1)
                nc.scalar.activation(long_i[0:1, g % 2:g % 2 + 1], excess_sum[:], ACT.Sign).then_inc(long_done, 1)

            def positive(g):
                act.wait_ge(fin_done, g + 1)
                wait(act, out_st[g % 2], 16 * (g // 2))
                nc.scalar.activation(y[:, g % 2, :, :].rearrange("p t c -> p (t c)"), misc[:], ACT.Relu).then_inc(relu_done, 1)

            def select(g):
                act.wait_ge(more_done, g + 1)
                act.wait_ge(rank_done, NQ * (g + 1))
                act.wait_ge(rank_dve, HQ)

                def item(chunk, level):
                    s = act.snap(sel, min_val=0, max_val=G * NQ * P)
                    wait_apart(act, sel_done, s + 1)
                    wait_apart(act, more_got, s + 1)
                    nc.scalar.activation(off_by[:, bass.ds(s % 2, 1), :], rank[:, g % 2, bass.ds(chunk, 1), :], ACT.Abs,
                                         bias=level_neg[:, bass.ds(level + STATIC, 1)]).then_inc(off_done, 1)
                    wait_apart(act, off_done, s + 1)
                    nc.scalar.activation(pick_more[:, bass.ds(s % SEL, 1), :], off_by[:, bass.ds(s % 2, 1), :], ACT.Relu,
                                         bias=one_t[:, 0:1], scale=-1.0).then_inc(sel_done, 1)
                    act.reg_add(sel, sel, 1)

                further_items(act, g % 2, chunks_with_more(act, g % 2), item)

            sel = act.alloc_register("act_sel")
            act.reg_mov(sel, 0)
            act.sem_inc(sel_done, 2)
            act.wait_ge(consts, CONSTS)
            deviation(0)
            for t in range(NT):
                absolute(0, t)
            for q in range(0, NQ, 2):
                mask(0, q, counted=2)
                if q == 2:
                    is_long(0)
            normalise(0)
            ranks(0, 0, counted=2)
            deviation(1)
            first_part(0)
            for t in range(NT):
                absolute(1, t)
                if t == 1:
                    second_part(0)
                if t + 1 < NT:
                    ranks(0, 2 * (t + 1), counted=2)
            for q in range(0, NQ, 2):
                mask(1, q, counted=2)
                if q < 4:
                    normalise(1, range(q, q + 2))
                if q == 4:
                    first_part(1)
            for t in range(NT):
                absolute(2, t)
                if t == 1:
                    second_part(1)

            for k in range(G):
                for q in range(NQ):
                    if q == 3 and k > 0:
                        positive(k - 1)
                    if q >= HQ and k + 1 < G:
                        ranks(k + 1, 2 * q - NQ)
                    if k + 2 < G:
                        mask(k + 2, q)
                    if q == 0:
                        for n in range(NP if k > 0 else 0):
                            start_maxima(k, n)
                        if k + 1 < G:
                            is_long(k + 1)
                    if q == 1 and 0 < k < G - 1:
                        first_part(k + 1)
                    if q == 2:
                        if 0 < k < G - 1:
                            second_part(k + 1)
                        select(k)
                    if q >= HQ and k + 1 < G:
                        ranks(k + 1, 2 * q - NQ + 1)
                    if q == 3:
                        turned_h(k)
                    if q in (1, 3, 4, 5) and k + 3 < G:
                        absolute(k + 3, (1, 3, 4, 5).index(q))
                    if k + 2 < G:
                        if q == 5:
                            deviation(k + 2)
                        if q >= NQ - 2:
                            first = 2 * (q - (NQ - 2))
                            normalise(k + 2, range(first, first + 2))
            positive(G - 1)

        @block.tensor
        def _(pe):
            pe.sem_inc(more_got, SEL)
            further = pe.alloc_register("pe_further")
            pe.reg_mov(further, 0)
            cuts = pe.alloc_register("pe_cuts")
            pe.reg_mov(cuts, 0)

            def transpose(g, q):
                pe.wait_ge(abs_done, NT * (g + 1))
                bank = flip
                if g >= 2:
                    pe.wait_ge(mask_done, NQ * g + q)
                elif q % 2 == 0:
                    wait(pe, mask_done, NQ * g + q)
                else:
                    wait(pe, mask_dve, HQ * g + q // 2)
                    bank = flip_odd
                for t in range(NT):
                    last = nc.tensor.transpose(bank[:, t * P:(t + 1) * P], adj_a[:, g % 2, t, q * P:(q + 1) * P], id_b[:])
                last.then_inc(flip_done, 1)

            def number(g, q):
                wait_masks(pe, g)
                bank = prefix
                if g > 0 or q % 2 == 0:
                    wait(pe, rank_done, NQ * g + q)
                else:
                    wait(pe, rank_dve, q // 2)
                    bank = prefix_odd
                nc.tensor.matmul(bank[:], tri_rank[:], maskT[:, g % 2, q, :], start=True, stop=True).then_inc(prefix_done, 1)

            def row_of_degrees(g):
                pe.wait_ge(tile_most, g + 1)
                wait(pe, hT_done, g - 1)
                nc.tensor.matmul(misc[0:1, 0:P], degree_most[:, 0:1], id_f[:], start=True, stop=True).then_inc(degree_row, 1)

            def count_row(g):
                pe.wait_ge(most_done, g + 1)
                pe.wait_ge(degree_read, min(g + 2, G))
                wait(pe, hT_done, g)
                nc.tensor.matmul(misc[0:1, 0:NQ * NT], most[:, 0:1], id_f[0:NQ * NT, 0:NQ * NT],
                                 start=True, stop=True).then_inc(most_row, 1)

            def cut(g):
                pe.wait_ge(long_done, g + 1)
                wait(pe, rank_done, NQ * g)
                with pe.If(pe.value_load(long_i[0:1, g % 2:g % 2 + 1], min_val=0, max_val=1)):
                    wait_masks(pe, g)
                    done = pe.snap(cuts, min_val=0, max_val=NQ * G)
                    for n, q in enumerate(range(NQ - 1, -1, -1)):
                        if n:
                            pe.wait_ge(cut_mask, done + n)
                        for before in range(q):
                            nc.tensor.matmul(prefix[:], ones_b[:], maskT[:, g % 2, before, :], start=(before == 0), stop=False)
                        nc.tensor.matmul(prefix[:], tri_cut[:], maskT[:, g % 2, q, :], start=(q == 0), stop=True).then_inc(cut_prefix, 1)
                    pe.wait_ge(cut_mask, done + NQ)
                    pe.reg_add(cuts, cuts, NQ)
                pe.nop()

            def gather(k, q, n):
                if q % HQ == 0 and n == 0:
                    pe.wait_ge(split_pool, 2 * (k - k % 2 + q // HQ + 1))
                if q > 0:
                    wait_taken(pe, k, q - 1, n)
                elif k > 0:
                    wait_taken(pe, k - 1, NQ - 1, n)
                for i in range(PAIR):
                    j = PAIR * n + i
                    if q % HQ == 0:
                        pe.wait_ge(pick_done, STATIC * (2 * k + q // HQ) + j + 1)
                    for part in range(PARTS):
                        last = nc.tensor.matmul(got[n][:, i, :], hpart[:, (k // 2) % 2, q, part, :], pick[:, q // HQ, j, q % HQ, :],
                                                start=(part == 0), stop=(part == PARTS - 1))
                last.then_inc(got_done, 1)

            def gather_more(k, active):
                pe.wait_ge(split_pool, 2 * (k - k % 2 + 2))

                def item(chunk, level):
                    d = pe.snap(further, min_val=0, max_val=G * NQ * P)
                    pe.wait_ge(sel_done, d + 3)
                    pe.wait_ge(more_max, d + 1)
                    for part in range(PARTS):
                        last = nc.tensor.matmul(got_more[:], hpart[:, (k // 2) % 2, bass.ds(chunk, 1), part, :].rearrange("p o c -> p (o c)"),
                                                pick_more[:, bass.ds(d % SEL, 1), :], start=(part == 0), stop=(part == PARTS - 1))
                    last.then_inc(more_got, 1)
                    pe.reg_add(further, further, 1)

                further_items(pe, k % 2, active, item)

            def turn_h(g):
                pe.wait_ge(h_done, NT * (g + 1))
                wait(pe, relu_done, g)
                pe.wait_ge(counts_done, g + 1)
                for t in range(NT):
                    last = nc.tensor.transpose(misc[:, t * P:(t + 1) * P], h32[:, g % 2, t, :], id_f[:])
                last.then_inc(hT_psum, 1)

            def finish(g):
                pe.wait_ge(agg_done, g + 1)
                pe.wait_ge(hT_done, min(g + 1, G))
                pe.wait_ge(counts_done, min(g + 2, G))
                if g == 0:
                    pe.wait_ge(w_in, 32)
                    pe.wait_ge(b_in, 16 * PARTS)
                nc.tensor.matmul(misc[:].rearrange("p (t c) -> p t c", t=NT), ones_b[0:PARTS, :],
                                 b_parts[:].unsqueeze(1).to_broadcast([PARTS, NT, C]), start=True, stop=False)
                for t in range(NT):
                    o = misc[:, t * P:(t + 1) * P]
                    nc.tensor.matmul(o, hT[:, g % 2, t * P:(t + 1) * P], w_t[:, 0, :], start=False, stop=False)
                    last = nc.tensor.matmul(o, agg[:, g % 2, t * P:(t + 1) * P], w_t[:, 1, :], start=False, stop=(t == NT - 1))
                last.then_inc(fin_done, 1)

            pe.wait_ge(consts, CONSTS)
            for q in range(NQ):
                transpose(0, q)
                if q == 2:
                    row_of_degrees(0)
            cut(0)
            for q in range(NQ):
                number(0, q)
            for q in range(NQ):
                transpose(1, q)

            for k in range(G):
                for q in range(NQ):
                    if q >= HQ and k + 1 < G:
                        number(k + 1, 2 * q - NQ)
                    if k + 2 < G and (k > 0 or q > 1):
                        transpose(k + 2, q)
                    gather(k, q, 0)
                    if k == 0 and q == 1:
                        transpose(2, 0)
                    if q >= HQ and k + 1 < G:
                        number(k + 1, 2 * q - NQ + 1)
                    if k + q == 0:
                        pe.wait_ge(mask_dve, 2 * HQ)
                        pe.wait_ge(rank_dve, HQ)
                    if q == 3:
                        pe.wait_ge(more_done, k + 1)
                        active = chunks_with_more(pe, k % 2)
                    gather(k, q, 1)
                    if k == 0 and q == 1:
                        transpose(2, 1)
                    if q == 3:
                        gather_more(k, active)
                    if q == 0 and k + 1 < G:
                        row_of_degrees(k + 1)
                    if q == 1:
                        count_row(k)
                    if q == 2 and k > 0:
                        finish(k - 1)
                    if q == 3:
                        turn_h(k)
                        if k + 1 < G:
                            cut(k + 1)
            finish(G - 1)

        @block.vector
        def _(dve):
            v = nc.vector
            dve.sem_inc(more_max, 1)
            further = dve.alloc_register("dve_further")
            dve.reg_mov(further, 0)
            cuts = dve.alloc_register("dve_cuts")
            dve.reg_mov(cuts, 0)

            def moments_of_tiles(g):
                if g == 0:
                    dve.wait_ge(x_first, 16)
                else:
                    dve.wait_ge(x_in, 16 * (max(g, 3) - 2))
                for t in range(NT):
                    v.bn_stats(stats[:, t, :], xs[:, g % XB, t, :]).then_inc(ln, 1)

            def moments(g):
                wait(dve, std_done, g)
                for t in range(NT):
                    dve.wait_ge(ln, LN_OPS * g + t + 1)
                    v.bn_aggr(mv[:, t, :], stats[:, t, :]).then_inc(ln, 1)

            def scale_bias(g):
                dve.wait_ge(std_done, g + 1)
                wait(dve, h_done, NT * g)
                v.reciprocal(rstd[:], std[:]).then_inc(ln, 1)
                dve.wait_ge(ln, LN_OPS * g + 2 * NT + 1)
                v.scalar_tensor_tensor(nmr[:], mv[:, :, 0], -1.0, rstd[:], ALU.mult, ALU.mult).then_inc(ln, 1)

            def picks(g, half, levels):
                dve.wait_ge(rank_done, NQ * g + HQ * (half + 1))
                dve.wait_ge(rank_dve, HQ // 2 * (half + 1) if g == 0 else HQ)
                wait(dve, got_done, NP * (NQ * (g - 1) + HQ * (half + 1)))
                for j in levels:
                    v.tensor_scalar(pick[:, half, j, :, :], rank[:, g % 2, HQ * half:HQ * (half + 1), :], MARK + j, None,
                                    ALU.is_equal).then_inc(pick_done, 1)

            def most_degree(g):
                dve.wait_ge(abs_done, NT * (g + 1))
                wait(dve, degree_row, g)
                v.reduce_max(degree_most[:], degree[:, g % 4, :], AX.X).then_inc(tile_most, 1)

            def most_in_chunks(g):
                dve.wait_ge(counting, 2 * g + 2)
                wait(dve, most_row, g)
                v.reduce_max(most[:, 0:1], in_chunk[:], AX.X).then_inc(most_done, 1)

            def count_of_chunks(g):
                dve.wait_ge(most_row, g + 1)
                wait(dve, key_step, KEY_OPS * g)
                v.reduce_max(counts[:], misc[0:1, 0:NQ * NT].rearrange("o (q t) -> o q t", t=NT), AX.X).then_inc(counts_done, 1)

            def sort_keys(g):
                dve.wait_ge(key_step, KEY_OPS * (g + 1))
                with nc.allow_low_precision(reason="a sum of NQ values 0 or 1"):
                    v.reduce_sum(more[0:1, g % 2, ACTIVE:ACTIVE + 1], some[:], AX.X)
                with nc.allow_low_precision(reason="a sum of NQ whole numbers up to P"):
                    v.reduce_sum(more[0:1, g % 2, TOTAL:TOTAL + 1], extra[:], AX.X)
                v.max(more[0:1, g % 2, KEYS:KEYS + NQ], keys[:]).then_inc(more_done, 1)

            def cut(g):
                dve.wait_ge(long_done, g + 1)
                with dve.If(dve.value_load(long_i[0:1, g % 2:g % 2 + 1], min_val=0, max_val=1)):
                    done = dve.snap(cuts, min_val=0, max_val=NQ * G)
                    for n, q in enumerate(range(NQ - 1, -1, -1)):
                        dve.wait_ge(cut_prefix, done + n + 1)
                        v.tensor_scalar(maskT[:, g % 2, q, :], prefix[:], CUT + KEEP - 1, None, ALU.is_le).then_inc(cut_mask, 1)
                    dve.reg_add(cuts, cuts, NQ)
                dve.nop()

            def first_maxima(n):
                dve.wait_ge(got_done, n + 1)
                v.tensor_copy(acc[:, 0, n, :, :], got[n][:]).then_inc(started, 1)

            def maxima(k, q, n):
                dve.wait_ge(got_done, NP * (NQ * k + q) + n + 1)
                wait_taken(dve, k, q - 1, n)
                v.tensor_tensor(acc[:, k % 2, n, :, :], acc[:, k % 2, n, :, :], got[n][:], ALU.max).then_inc(max_done, 1)

            def maxima_more(k, q, total):
                wait_taken(dve, k, q, NP - 1)

                with dve.If(total):
                    with dve.Fori(0, total) as _:
                        d = dve.snap(further, min_val=0, max_val=G * NQ * P)
                        dve.wait_ge(more_got, d + 1 + SEL)
                        dve.wait_ge(more_max, d + 1)
                        v.tensor_tensor(acc[:, k % 2, 0, 0, :], acc[:, k % 2, 0, 0, :], got_more[:], ALU.max).then_inc(more_max, 1)
                        dve.reg_add(further, further, 1)
                    dve.nop()
                dve.wait_ge(more_max, dve.snap(further, min_val=0, max_val=G * NQ * P) + 1)

            def join(k):
                a = acc[:, k % 2]
                wait_taken(dve, k, NQ - 1, NP - 1)
                v.tensor_tensor(a[:, 0], a[:, 0], a[:, 1], ALU.max).then_inc(joined, 1)
                dve.wait_ge(joined, k + 1)
                v.tensor_tensor(agg[:, k % 2, :], a[:, 0, 0], a[:, 0, 1], ALU.max).then_inc(agg_done, 1)

            def odd_mask(g, q):
                dve.wait_ge(flip_done, NQ * g + q + 1)
                v.tensor_scalar(maskT[:, g % 2, q, :], flip_odd, 0.0, None, ALU.is_gt).then_inc(mask_dve, 1)

            def odd_ranks(q):
                dve.wait_ge(prefix_done, q + 1)
                v.tensor_copy(rank[:, 0, q, :], prefix_odd).then_inc(rank_dve, 1)

            moments_of_tiles(0)
            moments(0)
            scale_bias(0)
            for q in range(1, NQ, 2):
                odd_mask(0, q)
                if q == 1:
                    most_degree(0)
            moments_of_tiles(1)
            moments(1)
            cut(0)
            for q in range(1, NQ, 2):
                odd_ranks(q)
            scale_bias(1)
            picks(0, 0, range(STATIC))
            for q in range(1, NQ, 2):
                odd_mask(1, q)
            most_degree(1)
            for k in range(G):
                for q in range(NQ):
                    if k + q == 0:
                        for n in range(NP):
                            first_maxima(n)
                    if q > 0:
                        maxima(k, q, 0)
                        if q == 2:
                            sort_keys(k)
                        if q == NQ - 1 and k + 1 < G:
                            picks(k + 1, 0, [2])
                        if q == 3:
                            dve.wait_ge(more_done, k + 1)
                            total = dve.value_load(more[0:1, k % 2, TOTAL:TOTAL + 1], min_val=0, max_val=NQ * P)
                        maxima(k, q, 1)
                    if q == 1:
                        count_of_chunks(k)
                    if q == 3:
                        maxima_more(k, q, total)
                    if q < HQ:
                        picks(k, 1, [q])
                    if q == 0:
                        most_in_chunks(k)
                    if q == 3 and k + 1 < G:
                        cut(k + 1)
                    if q == 3 and k + 2 < G:
                        moments_of_tiles(k + 2)
                    if q == 4 and k + 2 < G:
                        moments(k + 2)
                    if q == 5 and k + 2 < G:
                        scale_bias(k + 2)
                        most_degree(k + 2)
                    if q > HQ and k + 1 < G:
                        picks(k + 1, 0, {5: [0], 6: [1], 7: [3]}[q])
                join(k)


_INS = ['x', 'adj', 'L0_gnn_W', 'L0_gnn_b']
_OUTS = [((8, 1024, 128), 'float32')]


def kernel(**inputs):
    import numpy as _np
    import concourse.bacc as _bacc
    from concourse import mybir as _mybir
    from concourse.bass_utils import run_bass_kernel_spmd as _run

    nc = _bacc.Bacc("TRN2", target_bir_lowering=False, num_devices=1)
    arrays, args = {}, []
    for name in _INS:
        a = _np.ascontiguousarray(inputs[name])
        arrays[f"in_{name}_dram"] = a
        args.append(nc.dram_tensor(f"in_{name}_dram", a.shape, _mybir.dt.from_np(a.dtype), kind="ExternalInput").ap())
    for i, (shape, dtype) in enumerate(_OUTS):
        dt = _mybir.dt.from_np(_np.dtype(dtype))
        args.append(nc.dram_tensor(f"out_{i}_dram", shape, dt, kind="ExternalOutput").ap())
    gnn_layer(nc, *args)
    r = _run(nc, [arrays], core_ids=[0])
    got = tuple(r.results[0][f"out_{i}_dram"] for i in range(len(_OUTS)))
    return got[0]
```
